# Optimizing a Trainium2 kernel written in Bass

```python
import numpy as np
import jax
import jax.numpy as jnp

def _softmax(x, axis=-1):
    return jax.nn.softmax(x, axis=axis)

def _gelu(x):
    return jax.nn.gelu(x, approximate=True)

def _silu(x):
    return jax.nn.silu(x)

def _sigmoid(x):
    return jax.nn.sigmoid(x)

def _layernorm(x, axis=-1, eps=1e-05):
    m = jnp.mean(x, axis=axis, keepdims=True)
    v = jnp.var(x, axis=axis, keepdims=True)
    return (x - m) / jnp.sqrt(v + eps)

def _scatter_add(tgt, idx, src, axis=0):
    return tgt.at[idx].add(src)

def _segment_sum(src, seg, n):
    return jax.ops.segment_sum(src, seg, n)
kernel_name = 'mk_recurrent_d1_jaxref_r2_cd6356'

def setup_inputs(seed: int=0):
    np.random.seed(seed)
    _w = jnp.asarray

    def _L0_attn_setup():
        import jax, jax.numpy as jnp
        import numpy as np
        from jax.scipy.linalg import expm
        EPS = 1e-05

        def _layernorm(x, g, b):
            m = x.mean(-1, keepdims=True)
            v = ((x - m) ** 2).mean(-1, keepdims=True)
            return (x - m) / jnp.sqrt(v + EPS) * g + b
        H, S, K = (512, 64, 3)
        B, T = (4, 2048)
        key = jax.random.key(seed)
        ks = jax.random.split(key, 12)
        sc = 0.02
        inp = {'x': jax.random.normal(ks[0], (B, T, H), jnp.float32), 'A': -jnp.abs(jax.random.normal(ks[1], (S, S), jnp.float32) * sc), 'dt_A': jnp.asarray(0.1, jnp.float32), 'B_w': jax.random.normal(ks[2], (S, H), jnp.float32) * sc, 'B_b': jnp.zeros((S,), jnp.float32), 'C_w': jax.random.normal(ks[3], (S, H), jnp.float32) * sc, 'C_b': jnp.zeros((S,), jnp.float32), 'D_w': jax.random.normal(ks[4], (H, S), jnp.float32) * sc, 'D_b': jnp.zeros((H,), jnp.float32), 'conv_w': jax.random.normal(ks[5], (H, 1, K), jnp.float32) * sc, 'conv_b': jnp.zeros((H,), jnp.float32), 'gate_w': jax.random.normal(ks[6], (2 * H, H), jnp.float32) * sc, 'gate_b': jnp.zeros((2 * H,), jnp.float32), 'ln_in_g': jnp.ones((H,), jnp.float32), 'ln_in_b': jnp.zeros((H,), jnp.float32), 'ln_st_g': jnp.ones((S,), jnp.float32), 'ln_st_b': jnp.zeros((S,), jnp.float32)}
        return inp
    _L0_attn_in = _L0_attn_setup()

    def _L0_ffn_setup():
        import jax, jax.numpy as jnp
        import numpy as np
        key = jax.random.key(seed)
        k1, k2, k3, k4, k5 = jax.random.split(key, 5)
        d_in, d_out, r = (512, 512, 32)
        x = jax.random.normal(k1, (8, 4096, d_in), dtype=jnp.float32)
        W = jax.random.normal(k2, (d_out, d_in), dtype=jnp.float32) * (1.0 / np.sqrt(d_in))
        b = jax.random.normal(k3, (d_out,), dtype=jnp.float32) * 0.01
        V_r = jax.random.normal(k4, (d_in, r), dtype=jnp.float32) * (1.0 / np.sqrt(d_in))
        C = jax.random.normal(k5, (d_out, r), dtype=jnp.float32) * (1.0 / np.sqrt(r))
        return {'x': x, 'W': W, 'b': b, 'V_r': V_r, 'C': C}
    _L0_ffn_in = _L0_ffn_setup()
    _d = {'L0_attn_x': _L0_attn_in['x'], 'L0_attn_A': _L0_attn_in['A'], 'L0_attn_dt_A': _L0_attn_in['dt_A'], 'L0_attn_B_w': _L0_attn_in['B_w'], 'L0_attn_B_b': _L0_attn_in['B_b'], 'L0_attn_C_w': _L0_attn_in['C_w'], 'L0_attn_C_b': _L0_attn_in['C_b'], 'L0_attn_D_w': _L0_attn_in['D_w'], 'L0_attn_D_b': _L0_attn_in['D_b'], 'L0_attn_conv_w': _L0_attn_in['conv_w'], 'L0_attn_conv_b': _L0_attn_in['conv_b'], 'L0_attn_gate_w': _L0_attn_in['gate_w'], 'L0_attn_gate_b': _L0_attn_in['gate_b'], 'L0_attn_ln_in_g': _L0_attn_in['ln_in_g'], 'L0_attn_ln_in_b': _L0_attn_in['ln_in_b'], 'L0_attn_ln_st_g': _L0_attn_in['ln_st_g'], 'L0_attn_ln_st_b': _L0_attn_in['ln_st_b'], 'L0_ffn_W': _L0_ffn_in['W'], 'L0_ffn_b': _L0_ffn_in['b'], 'L0_ffn_V_r': _L0_ffn_in['V_r'], 'L0_ffn_C': _L0_ffn_in['C']}
    _x0 = _d['L0_attn_x']
    _d['L0_attn_x'] = jax.random.normal(jax.random.fold_in(jax.random.key(seed), 1), (8, 2048, 512), dtype=_x0.dtype)
    del _x0
    return _d

def reference(L0_attn_x, L0_attn_A, L0_attn_dt_A, L0_attn_B_w, L0_attn_B_b, L0_attn_C_w, L0_attn_C_b, L0_attn_D_w, L0_attn_D_b, L0_attn_conv_w, L0_attn_conv_b, L0_attn_gate_w, L0_attn_gate_b, L0_attn_ln_in_g, L0_attn_ln_in_b, L0_attn_ln_st_g, L0_attn_ln_st_b, L0_ffn_W, L0_ffn_b, L0_ffn_V_r, L0_ffn_C):

    def _L0_attn_ref(x, A, dt_A, B_w, B_b, C_w, C_b, D_w, D_b, conv_w, conv_b, gate_w, gate_b, ln_in_g, ln_in_b, ln_st_g, ln_st_b):
        import jax, jax.numpy as jnp
        import numpy as np
        from jax.scipy.linalg import expm
        EPS = 1e-05

        def _layernorm(x, g, b):
            m = x.mean(-1, keepdims=True)
            v = ((x - m) ** 2).mean(-1, keepdims=True)
            return (x - m) / jnp.sqrt(v + EPS) * g + b
        Bt, T, H = x.shape
        K = conv_w.shape[-1]
        pad = K // 2
        x_norm = _layernorm(x, ln_in_g, ln_in_b)
        xc = jnp.transpose(x_norm, (0, 2, 1))
        xc = jax.lax.conv_general_dilated(xc, conv_w, window_strides=(1,), padding=[(pad, pad)], dimension_numbers=('NCH', 'OIH', 'NCH'), feature_group_count=H)
        xc = xc + conv_b[None, :, None]
        x_norm = x_norm + jnp.transpose(xc, (0, 2, 1))
        gate_all = x_norm @ gate_w.T + gate_b
        gate, input_gate = (gate_all[..., :H], gate_all[..., H:])
        gate = jax.nn.sigmoid(gate)
        Bm = x_norm * jax.nn.sigmoid(input_gate) @ B_w.T + B_b
        Cm = x_norm @ C_w.T + C_b
        A_bar = expm(dt_A * A)

        def step(state, bc):
            b_t, c_t = bc
            s = state @ A_bar + b_t
            s = _layernorm(s, ln_st_g, ln_st_b)
            return (s, c_t * s)
        state0 = jnp.zeros((Bt, A.shape[0]), x.dtype)
        _, ys = jax.lax.scan(step, state0, (jnp.transpose(Bm, (1, 0, 2)), jnp.transpose(Cm, (1, 0, 2))))
        ssm = jnp.transpose(ys, (1, 0, 2))
        ssm = ssm @ D_w.T + D_b
        return ssm * gate

    def _L0_ffn_ref(x, W, b, V_r, C):
        import jax, jax.numpy as jnp
        import numpy as np
        base = jnp.einsum('bsd,od->bso', x, W) + b
        correction = jnp.einsum('bsr,or->bso', jnp.einsum('bsd,dr->bsr', x, V_r), C)
        return base + correction
    x = L0_attn_x
    xn = _layernorm(x, axis=-1)
    s = _L0_attn_ref(xn, L0_attn_A, L0_attn_dt_A, L0_attn_B_w, L0_attn_B_b, L0_attn_C_w, L0_attn_C_b, L0_attn_D_w, L0_attn_D_b, L0_attn_conv_w, L0_attn_conv_b, L0_attn_gate_w, L0_attn_gate_b, L0_attn_ln_in_g, L0_attn_ln_in_b, L0_attn_ln_st_g, L0_attn_ln_st_b)
    g = _silu(_L0_ffn_ref(xn, L0_ffn_W, L0_ffn_b, L0_ffn_V_r, L0_ffn_C))
    x = x + s * g
    return x

_drawn_inputs = setup_inputs


def setup_inputs(seed=0):
    import zlib

    import numpy as np

    out = dict(_drawn_inputs(seed))
    spreads = {'L0_attn_B_b': (0.0, 1.356),
     'L0_attn_C_b': (0.0, 0.482),
     'L0_attn_D_b': (0.0, 0.1),
     'L0_attn_conv_b': (0.0, 0.8),
     'L0_attn_gate_b': (0.0, 2.0),
     'L0_attn_ln_in_g': (1.0, 0.6),
     'L0_attn_ln_in_b': (0.0, 0.8),
     'L0_attn_ln_st_g': (1.0, 0.586),
     'L0_attn_ln_st_b': (0.0, 0.556)}
    factors = {'L0_attn_A': 64.0,
     'L0_attn_B_w': 3.975,
     'L0_attn_conv_w': 8.0,
     'L0_attn_gate_w': 3.423,
     'L0_ffn_b': 64.0}
    for name, (base, spread) in spreads.items():
        noise = np.random.default_rng([zlib.crc32(name.encode()), seed]).standard_normal(out[name].shape)
        drawn = base * np.exp(spread * noise) if base else spread * noise
        out[name] = jnp.asarray(drawn.astype(out[name].dtype))
    for name, factor in factors.items():
        out[name] = (out[name] * factor).astype(out[name].dtype)
    return out
```

```python
from contextlib import ExitStack

import numpy as np

import concourse.bass as bass
from concourse import mybir

ALU = mybir.AluOpType
ACT = mybir.ActivationFunctionType
F32 = mybir.dt.float32
I32 = mybir.dt.int32
AX_X = mybir.AxisListType.X

P = 128
B = 8
T = 2048
H = 512
S = 64
R = 32
KH = H // P
CT = 64
NC = T // CT
TOK = B * CT
NJ = TOK // P
BJ = B // NJ
EPS = 1e-5
SQUARINGS = 20
TERMS = 12

OUT = ["out_even", "out_odd"]

VEC = ["ln_g", "ln_b", "conv_w0", "conv_w1", "conv_w2", "conv_b", "gate_b", "in_gate_b", "ffn_b", "D_b"]
SMALL = {"A": (0, S), "AT": (S, S), "st_g": (2 * S, 1), "st_b": (2 * S + 1, 1), "C_b": (2 * S + 2, 1),
         "dt": (2 * S + 3, 1), "pow": (2 * S + 4, SQUARINGS), "inv": (2 * S + 4 + SQUARINGS, SQUARINGS)}
SMALL_W = 2 * S + 4 + 2 * SQUARINGS

T_USERS = [("wr", 0, "C")] + [("z", k, "A") for k in range(KH)] + [("x", k, "A") for k in range(KH)] \
    + [("o", j, "C") for j in range(NJ)] + [("d", 0, "A")]
M_USERS = [("ffn", m, "F") for m in range(KH)] + [("ssm", m, "C") for m in range(KH)] \
    + [("gate", m, "F") for m in range(3)] + [("ig", m, "A") for m in range(KH)] \
    + [("b", 0, "A"), ("gate", 3, "F"), ("c", 0, "A")]

PE_FFN = range(0, 16)
PE_W = range(10, 14)
PE_SSM = range(16, 20)
PE_Z = (20, 20, 22, 22)
PE_X = (27, 27, 29, 29)
PE_GATE = (21, 23, 24, 25) + (26, 28, 30, 31) + (32, 33, 34, 35) + (56, 57, 58, 59)
PE_O = range(30, 46)
PE_IG = range(36, 52)
PE_B = range(52, 56)
PE_D = 57
PE_C = range(60, 64)
V_STATS = range(0, 4)
V_AGGR = 4
V_SILU = (5, 9, 13, 17)
V_YS = 15
V_SG = range(18, 22)
V_CONV = range(23, 31)
V_G = (31, 33, 37, 61)
V_ADD = (35, 39, 43, 47)
V_XG = (41, 45, 49, 53)
POOL_RS = (5, 6, 7)
POOL_LN = (8, 8, 9, 10, 11, 12, 13, 14, 15, 16, 16, 17)


def build(nc, x, ident_d, gateT_d, WT_d, VT_d, CrT_d, BT_d, CwT_d, DT_d, vec_d, small_d, Bb_d, out):
    with ExitStack() as ctx:
        def sb(name, shape, dt=F32):
            return ctx.enter_context(nc.sbuf_tensor(name, shape, dt))

        def sem(name):
            return ctx.enter_context(nc.semaphore(name))

        ident = sb("ident", [P, P])
        gateT = sb("gateT", [P, KH, 2 * H])
        WT = sb("WT", [P, KH, H])
        VT = sb("VT", [R, H])
        CrT = sb("CrT", [R, H])
        BT = sb("BT", [P, KH, S])
        CwT = sb("CwT", [P, KH, S])
        DT = sb("DT", [S, H])
        vec = sb("vec", [P, len(VEC), KH])
        small = sb("small", [S, SMALL_W])
        Bb = sb("Bb", [1, S])
        ones = sb("ones", [1, P])
        minus_half = sb("minus_half", [P, NJ])
        dbias = sb("dbias", [S, 1])
        btmp = sb("btmp", [P, KH])
        As = sb("As", [S, 2, S])
        absrow = sb("absrow", [S, 8])
        XX = sb("XX", [S, 2, S])
        mask = sb("mask", [S, SQUARINGS])
        pick = sb("pick", [S, SQUARINGS])
        AC = sb("AC", [S, S])
        M = sb("M", [S, S])
        M2 = sb("M2", [32, 2, S])
        st_b_wide = sb("st_b_wide", [S, P])
        xa = sb("xa", [P, NJ, H])
        xc = sb("xc", [P, NJ, H])
        stats = sb("stats", [P, NJ, 6])
        mv = sb("mv", [P, NJ, 2])
        ln = sb("ln", [P, 8, NJ])
        z = sb("z", [P, NJ, H])
        y = sb("y", [P, KH, B, CT + 2])
        halo = sb("halo", [P, KH, B, 2, NC])
        xnT = sb("xnT", [P, KH, TOK])
        xnorm = [sb(f"xnorm{p}", [P, KH, TOK]) for p in range(2)]
        xg = sb("xg", [P, KH, TOK])
        sigf = sb("sigf", [P, 2, TOK])
        G = [sb(f"G{p}", [P, KH, TOK]) for p in range(2)]
        cT = [sb(f"cT{p}", [S, TOK]) for p in range(2)]
        dT = sb("dT", [S, TOK])
        dtok = sb("dtok", [P, NJ, S])
        dw = [sb(f"dw{p}", [32, CT, S]) for p in range(2)]
        wtok = sb("wtok", [P, NJ, S])
        wsq = sb("wsq", [P, NJ, S])
        ssq = sb("ssq", [P, 3, NJ])
        wr = sb("wr", [P, NJ, S])
        ys = sb("ys", [S, TOK])
        sgT = sb("sgT", [P, KH, TOK])
        o = sb("o", [P, 2, H])
        wT = sb("wT", [32, S])
        wq = sb("wq", [B, S])
        q = sb("q", [B, 1])
        r = sb("r", [B, 1])

        banks = [ctx.enter_context(nc.psum_tensor(f"bank{n}", [P, TOK], F32)) for n in range(8)]
        scanP = banks[0]
        tbank = {}
        for n, (what, k, _) in enumerate(T_USERS):
            tbank[what, k] = banks[1 + n % 2]
        mbank = {}
        for n, (what, k, _) in enumerate(M_USERS):
            mbank[what, k] = banks[[3, 4, 7][n % 3]]
        cbank = [banks[5], banks[6]]
        wbank = [banks[3], banks[4], banks[7], banks[3]]

        names = """held consts weights_in halo_in xa_in xc_in d_in w_in out_even out_odd dve_cleared pool_cleared pe_setup dve_setup halo_zeroed xc_cleared m2_in wprime_mm wprime_done
            p_ready r_ready w_ready q_ready wT_ready
            stats_done mv_done ln_done z_done zfill y_done halo_y t1_done conv_half xnorm_done xn_done xfill xnT_done
            ig_mm igs_done xg_done b_mm dT_done dfill dtok_done c_mm cT_done
            ffn_mm sigf_done silu_done gate_mm gates_done g_done
            ssq_done rs_done wr_done wrfill sn_done ys_done ssm_mm sg_done ofill o_done""".split()
        s = {n: sem(n) for n in names}

        vcol = {n: i for i, n in enumerate(VEC)}

        def v_(name, k):
            return vec[:, vcol[name], k:k + 1]

        def sm(name):
            a, w = SMALL[name]
            return small[:, a:a + w]

        def released(user, i):
            what, k = user
            return {
                "z": lambda: ("y_done", KH, i + 2, k + 1),
                "x": lambda: ("xnT_done", KH, i + 1, k + 1),
                "wr": lambda: ("ys_done", 1, i, 0),
                "o": lambda: ("o_done", NJ, i - 1, k + 1),
                "ffn": lambda: ("silu_done", KH, i, k + 1),
                "gate": lambda: ("g_done", KH, i, k + 1),
                "ssm": lambda: ("sg_done", KH, i - 1, k + 1),
                "ig": lambda: ("xg_done", KH, i + 1, k + 1),
                "b": lambda: ("dT_done", 1, i + 1, 1),
                "d": lambda: ("dtok_done", 1, i + 1, 1),
                "c": lambda: ("cT_done", 1, i + 1, 1),
            }[what]()

        def parts_of(i, middle):
            if middle:
                return "AFC"
            return {-2: "z", -1: "A", 0: "AF", NC - 1: "FC", NC: "C"}.get(i, "AFC" if 0 < i < NC else "")

        def wait_for(eng, name, per, n, k):
            v = n * per + k
            if isinstance(v, int) and v <= 0:
                return
            eng.wait_ge(s[name], v)

        def hold(eng):
            eng.sem_inc(s["held"], 1)

        def wait_bank(eng, users, what, k, i, middle):
            n = [u[:2] for u in users].index((what, k))
            size = 2 if users is T_USERS else 3
            back, at = 0, n
            while back < 4:
                at -= 1
                if at < 0:
                    at, back = len(users) - 1, back + 1
                same = at % size == n % size
                parts = parts_of(i if middle else i - back, middle)
                here = users[at][2] in parts or (parts == "z" and users[at][0] == "z")
                if same and here:
                    wait_for(eng, *released(users[at][:2], i - back))
                    return

        block = ctx.enter_context(nc.Block())

        @block.sync
        def _(sp):
            def load_x(dst, c, name):
                for b in range(B):
                    sp.dma_start(dst[CT * (b % BJ):CT * (b % BJ) + CT, b // BJ, :],
                                 x[b, bass.ds(c * CT, CT), :]).then_inc(s[name], 16)

            for dst, src in [(small[:], small_d), (ident[:], ident_d), (vec[:], vec_d), (Bb[:], Bb_d)]:
                sp.dma_start(dst, src).then_inc(s["consts"], 16)
            load_x(xa, 0, "xa_in")
            sp.wait_ge(s["xc_cleared"], 1)
            for b in range(B):
                p0 = CT * (b % BJ)
                for a, e in ((1, NC // 2 + 1), (NC // 2 + 1, NC)):
                    sp.dma_start(xc[p0 + a:p0 + e, b // BJ, :],
                                 x[b, CT * a - 1:CT * (e - 1):CT, :]).then_inc(s["halo_in"], 16)
                for a, e in ((0, NC // 2), (NC // 2, NC - 1)):
                    sp.dma_start(xc[p0 + NC + a:p0 + NC + e, b // BJ, :],
                                 x[b, CT * (a + 1):CT * e + 1:CT, :]).then_inc(s["halo_in"], 16)
            for dst, src in [(BT[:], BT_d.rearrange("(k p) n -> p k n", p=P)), (VT[:], VT_d), (CrT[:], CrT_d),
                             (WT[:], WT_d.rearrange("(k p) n -> p k n", p=P)),
                             (gateT[:], gateT_d.rearrange("(k p) n -> p k n", p=P)),
                             (CwT[:], CwT_d.rearrange("(k p) n -> p k n", p=P)), (DT[:], DT_d)]:
                sp.dma_start(dst, src).then_inc(s["weights_in"], 16)

            def send_d(c, p):
                if isinstance(c, int) and c == 0:
                    sp.wait_ge(s["pool_cleared"], 2)
                wait_for(sp, "dtok_done", 1, c, 1)
                hold(sp)
                wait_for(sp, "w_in", 16 * B, c - 1, 0)
                for b in range(B):
                    sp.dma_start(dw[p][b:b + 1, :, :],
                                 dtok[CT * (b % BJ):CT * (b % BJ) + CT, b // BJ, :]).then_inc(s["d_in"], 16)

            def send_w(c, p):
                wait_for(sp, "w_ready", CT, c, CT)
                hold(sp)
                wait_for(sp, "wr_done", NJ, c, 0)
                for b in range(B):
                    sp.dma_start(wtok[CT * (b % BJ):CT * (b % BJ) + CT, b // BJ, :],
                                 dw[p][b:b + 1, :, :]).then_inc(s["w_in"], 16)

            def prefetch_xa(c):
                wait_for(sp, "xn_done", NJ, c, 0)
                hold(sp)
                load_x(xa, c, "xa_in")

            def send_out(c, j):
                wait_for(sp, "o_done", NJ, c, j + 1)
                hold(sp)
                for b in range(BJ):
                    sp.dma_start(out[BJ * j + b, bass.ds(c * CT, CT), :],
                                 o[CT * b:CT * b + CT, j % 2, :]).then_inc(s[OUT[j % 2]], 16)

            sp.wait_ge(s["dve_setup"], SETUP_M - 7)
            for h in range(2):
                sp.dma_start(M2[:, h, :], M[32 * h:32 * h + 32, :]).then_inc(s["m2_in"], 16)
            prefetch_xa(1)
            send_d(0, 0)

            def iteration(i, p, parts, middle):
                if "C" in parts:
                    send_w(i - 1, 1 - p)
                if "A" in parts and (middle or i + 2 < NC):
                    prefetch_xa(i + 2)
                if "C" in parts:
                    for j in range(NJ):
                        send_out(i - 1, j)
                if "F" in parts:
                    wait_for(sp, "z_done", NJ, i, NJ)
                    hold(sp)
                    wait_for(sp, "o_done", NJ, i, 0)
                    hold(sp)
                    load_x(xc, i, "xc_in")
                if "A" in parts:
                    send_d(i + 1, 1 - p)

            iteration(0, 0, "AF", False)
            iteration(1, 1, "AFC", False)
            with sp.Fori(1, NC // 2 - 1) as pair:
                i = sp.snap(2 * pair)
                iteration(i, 0, "AFC", True)
                iteration(i + 1, 1, "AFC", True)
            iteration(NC - 2, 0, "AFC", False)
            iteration(NC - 1, 1, "FC", False)
            iteration(NC, 0, "C", False)
            for name in OUT:
                sp.wait_ge(s[name], 8 * B * NC)

        @block.gpsimd
        def _(pool):
            nc.gpsimd.memset(minus_half[:], -0.5).then_inc(s["pool_cleared"], 1)
            nc.gpsimd.memset(dw[0][:], 0.0)
            nc.gpsimd.memset(dw[1][:], 0.0).then_inc(s["pool_cleared"], 1)
            pool.wait_ge(s["pool_cleared"], 2)
            pool.wait_ge(s["dve_cleared"], 1)

            def step(i, t):
                wait_for(pool, "q_ready", CT, i, t + 1)
                nc.gpsimd.tensor_tensor(r[:], q[:], minus_half[0:B, 0:1], ALU.pow).then_inc(s["r_ready"], 1)

            def ln_op(n, k):
                mean, var = mv[:, :, 0], mv[:, :, 1]
                nm, a, r1, v2, r2, rr, bx, bz = (ln[:, a, :] for a in range(8))
                if k == 0:
                    wait_for(pool, "mv_done", NJ, n, NJ)
                    wait_for(pool, "xn_done", NJ, n - 1, 0)
                    wait_for(pool, "z_done", NJ, n, 0)
                else:
                    wait_for(pool, "ln_done", LN_OPS, n, k)
                hold(pool)
                g = nc.gpsimd
                ins = [
                    lambda: g.tensor_scalar(nm, mean, -1.0, None, ALU.mult),
                    lambda: g.tensor_scalar(a, var, EPS, None, ALU.add),
                    lambda: g.tensor_tensor(r1[:, 0:2], a[:, 0:2], minus_half[:, 0:2], ALU.pow),
                    lambda: g.tensor_tensor(r1[:, 2:4], a[:, 2:4], minus_half[:, 2:4], ALU.pow),
                    lambda: g.tensor_tensor(v2, var, r1, ALU.mult),
                    lambda: g.tensor_tensor(v2, v2, r1, ALU.mult),
                    lambda: g.tensor_scalar(a, v2, EPS, None, ALU.add),
                    lambda: g.tensor_tensor(r2[:, 0:2], a[:, 0:2], minus_half[:, 0:2], ALU.pow),
                    lambda: g.tensor_tensor(r2[:, 2:4], a[:, 2:4], minus_half[:, 2:4], ALU.pow),
                    lambda: g.tensor_tensor(rr, r1, r2, ALU.mult),
                    lambda: g.tensor_tensor(bx, nm, r1, ALU.mult),
                    lambda: g.tensor_tensor(bz, nm, rr, ALU.mult),
                ][k]()
                ins.then_inc(s["ln_done"], 1)

            def state_scale(c, k):
                if k == 0:
                    wait_for(pool, "ssq_done", NJ, c, NJ)
                    hold(pool)
                    nc.gpsimd.tensor_scalar(ssq[:, 1, :], ssq[:, 0, :], EPS, None,
                                            ALU.add).then_inc(s["rs_done"], 1)
                else:
                    wait_for(pool, "rs_done", 3, c, k)
                    wait_for(pool, "wr_done", NJ, c, 0)
                    half = slice(2 * k - 2, 2 * k)
                    nc.gpsimd.tensor_tensor(ssq[:, 2, half], ssq[:, 1, half], minus_half[:, half],
                                            ALU.pow).then_inc(s["rs_done"], 1)

            for n in range(2):
                for k in range(LN_OPS):
                    ln_op(n, k)

            def iteration(i, parts):
                for t in range(CT):
                    if "F" in parts:
                        step(i, t)
                    if "C" in parts and t in POOL_RS:
                        state_scale(i - 1, POOL_RS.index(t))
                    if "A" in parts:
                        for k in range(LN_OPS):
                            if POOL_LN[k] == t:
                                ln_op(i + 2, k)

            iteration(0, "AF")
            iteration(1, "AFC")
            with pool.Fori(1, NC // 2 - 1) as pair:
                i = pool.snap(2 * pair)
                iteration(i, "AFC")
                iteration(i + 1, "AFC")
            iteration(NC - 2, "AFC")
            iteration(NC - 1, "FC")
            iteration(NC, "C")

        @block.scalar
        def _(act):
            a_ = nc.scalar.activation

            def normalise_z(n, src=xa):
                wait_for(act, "ln_done", LN_OPS, n, LN_OPS)
                wait_for(act, "xfill", KH, n - 1, 0)
                for j in range(NJ):
                    a_(z[:, j, :], src[:, j, :], ACT.Identity, bias=ln[:, 7, j:j + 1],
                       scale=ln[:, 5, j:j + 1]).then_inc(s["z_done"], 1)

            def normalise_x(c, tiles):
                if tiles[0] == 0:
                    wait_for(act, "zfill", KH, c + 1, KH)
                for j in tiles:
                    a_(z[:, j, :], xa[:, j, :], ACT.Identity, bias=ln[:, 6, j:j + 1],
                       scale=ln[:, 2, j:j + 1]).then_inc(s["xn_done"], 1)

            def make_y(c, k):
                wait_for(act, "zfill", KH, c + 1, k + 1)
                wait_for(act, "xnorm_done", KH, c - 1, k + 1)
                a_(y[:, k, :, 1:CT + 1], tbank["z", k][:].rearrange("p (b t) -> p b t", b=B),
                   ACT.Identity, bias=v_("ln_b", k), scale=v_("ln_g", k)).then_inc(s["y_done"], 1)

            def copy_halo(c):
                wait_for(act, "xnorm_done", KH, c, 0)
                nc.scalar.copy(y[:, :, :, 0:CT + 2:CT + 1],
                               halo[:, :, :, :, bass.ds(c, 1)].rearrange("p k b s o -> p k b (s o)")
                               ).then_inc(s["halo_y"], 1)

            def centre_tap(c, k):
                wait_for(act, "y_done", KH, c + 1, k + 1)
                wait_for(act, "xnorm_done", KH, c, k - 1)
                a_(cbank[k % 2][:].rearrange("p (b t) -> p b t", b=B), y[:, k, :, 1:CT + 1],
                   ACT.Identity, bias=v_("conv_b", k), scale=v_("conv_w1", k)).then_inc(s["t1_done"], 1)

            def copy_xnT(c, k):
                wait_for(act, "xfill", KH, c, k + 1)
                wait_for(act, "ffn_mm", KH, c, 0)
                nc.scalar.copy(xnT[:, k, :], tbank["x", k][:]).then_inc(s["xnT_done"], 1)

            def input_gate(c, m):
                wait_for(act, "ig_mm", KH, c, m + 1)
                a_(mbank["ig", m][:], mbank["ig", m][:], ACT.Sigmoid,
                   bias=v_("in_gate_b", m)).then_inc(s["igs_done"], 1)

            def copy_c(c, p):
                wait_for(act, "c_mm", 1, c, 1)
                wait_for(act, "ys_done", 1, c - 1, 0)
                a_(cT[p][:], mbank["c", 0][0:S, :], ACT.Identity, bias=sm("C_b")).then_inc(s["cT_done"], 1)

            def copy_dT(c):
                wait_for(act, "b_mm", 1, c, 1)
                a_(dT[:], mbank["b", 0][0:S, :], ACT.Identity, bias=dbias[:]).then_inc(s["dT_done"], 1)

            def copy_dtok(c):
                wait_for(act, "dfill", 1, c, 1)
                wait_for(act, "d_in", 16 * B, c, 0)
                nc.scalar.copy(dtok[:].rearrange("p j e -> p (j e)"),
                               tbank["d", 0][:, 0:NJ * S]).then_inc(s["dtok_done"], 1)

            def ffn_sigmoid(c, m):
                wait_for(act, "ffn_mm", KH, c, m + 1)
                wait_for(act, "silu_done", KH, c, m - 1)
                a_(sigf[:, m % 2, :], mbank["ffn", m][:], ACT.Sigmoid,
                   bias=v_("ffn_b", m)).then_inc(s["sigf_done"], 1)

            def gate_sigmoid(c, m):
                wait_for(act, "gate_mm", KH, c, m + 1)
                a_(mbank["gate", m][:], mbank["gate", m][:], ACT.Sigmoid,
                   bias=v_("gate_b", m)).then_inc(s["gates_done"], 1)

            def state_squares(c):
                wait_for(act, "w_in", 16 * B, c, 16 * B)
                wait_for(act, "rs_done", 3, c, 0)
                for j in range(NJ):
                    a_(wsq[:, j, :], wtok[:, j, :], ACT.Square, scale=float(S) ** -0.5,
                       accum_out=ssq[:, 0, j:j + 1]).then_inc(s["ssq_done"], 1)

            def state_normalise(c):
                wait_for(act, "rs_done", 3, c, 3)
                wait_for(act, "wrfill", 1, c, 0)
                for j in range(NJ):
                    a_(wr[:, j, :], wtok[:, j, :], ACT.Copy,
                       scale=ssq[:, 2, j:j + 1]).then_inc(s["wr_done"], 1)

            def state_affine(c):
                wait_for(act, "wrfill", 1, c, 1)
                bank = tbank["wr", 0][0:S, :]
                a_(bank, bank, ACT.Identity, bias=sm("st_b"), scale=sm("st_g")).then_inc(s["sn_done"], 1)

            act.wait_ge(s["consts"], 16 * 4)
            act.wait_ge(s["dve_setup"], SETUP_VEC)
            normalise_z(0, xc)
            for k in range(KH):
                act.wait_ge(s["zfill"], k + 1)
                a_(halo[:, k].rearrange("p b s c -> p (b s c)"), tbank["z", k][:], ACT.Identity,
                   bias=v_("ln_b", k), scale=v_("ln_g", k)).then_inc(s["y_done"], 1)
            normalise_z(1)

            def part_a(c):
                for k in range(2):
                    make_y(c, k)
                for k in range(2):
                    centre_tap(c, k)
                for k in range(2, 4):
                    make_y(c, k)
                normalise_x(c, (0, 1))
                centre_tap(c, 2)
                normalise_x(c, (2, 3))

            def part_b(c):
                centre_tap(c, 3)
                for k in range(KH):
                    copy_xnT(c, k)

            act.wait_ge(s["halo_zeroed"], 1)
            copy_halo(0)
            part_a(0)
            part_b(0)
            for m in range(KH):
                input_gate(0, m)
            act.wait_ge(s["dve_setup"], SETUP_M + 1)
            copy_dT(0)
            copy_dtok(0)
            copy_c(0, 0)

            def iteration(i, p, parts):
                A, F, C = ("A" in parts), ("F" in parts), ("C" in parts)
                if C:
                    state_squares(i - 1)
                if F:
                    ffn_sigmoid(i, 0)
                if C:
                    state_normalise(i - 1)
                if F:
                    ffn_sigmoid(i, 1)
                    ffn_sigmoid(i, 2)
                if C:
                    state_affine(i - 1)
                if F:
                    ffn_sigmoid(i, 3)
                if A:
                    normalise_z(i + 2)
                    copy_halo(i + 1)
                    part_a(i + 1)
                if F:
                    gate_sigmoid(i, 0)
                if A:
                    part_b(i + 1)
                if F:
                    gate_sigmoid(i, 1)
                    gate_sigmoid(i, 2)
                if A:
                    for m in range(KH):
                        input_gate(i + 1, m)
                    copy_dT(i + 1)
                    copy_dtok(i + 1)
                if F:
                    gate_sigmoid(i, 3)
                if A:
                    copy_c(i + 1, 1 - p)

            iteration(0, 0, "AF")
            iteration(1, 1, "AFC")
            with act.Fori(1, NC // 2 - 1) as pair:
                i = act.snap(2 * pair)
                iteration(i, 0, "AFC")
                iteration(i + 1, 1, "AFC")
            iteration(NC - 2, 0, "AFC")
            iteration(NC - 1, 1, "FC")
            iteration(NC, 0, "C")

        @block.vector
        def _(dve):
            done = [0]

            def link(ins):
                done[0] += 1
                ins.then_inc(s["dve_setup"], 1)
                dve.wait_ge(s["dve_setup"], done[0])

            V = nc.vector
            V.memset(xc[:], 0.0).then_inc(s["xc_cleared"], 1)
            V.memset(ones[:], 1.0)
            V.memset(wT[:], 0.0)
            V.memset(st_b_wide[:], 1.0)
            V.memset(r[:], -1.0).then_inc(s["dve_cleared"], 1)
            dve.wait_ge(s["consts"], 16 * 4)
            dve.wait_ge(s["dve_cleared"], 1)

            def row_stats(n, src):
                for j in range(NJ):
                    V.bn_stats(stats[:, j, :], src[:, j, :]).then_inc(s["stats_done"], 1)
                aggregate(n)

            def bn_stats(n, j):
                if j == 0:
                    wait_for(dve, "xa_in", 16 * B, n, 0)
                V.bn_stats(stats[:, j, :], xa[:, j, :]).then_inc(s["stats_done"], 1)

            def aggregate(n):
                wait_for(dve, "stats_done", NJ, n, NJ)
                wait_for(dve, "ln_done", LN_OPS, n, 0)
                hold(dve)
                for j in range(NJ):
                    V.bn_aggr(mv[:, j, :], stats[:, j, :]).then_inc(s["mv_done"], 1)

            link(V.tensor_scalar(vec[:, vcol["conv_w1"], :], vec[:, vcol["conv_w1"], :], 1.0, None, ALU.add))
            assert done[0] == SETUP_VEC
            link(V.tensor_scalar(As[:].rearrange("p a b -> p (a b)"), small[:, 0:2 * S], sm("dt"), None, ALU.mult))
            link(V.tensor_reduce(absrow[:, 0:1], As[:, 0, :], AX_X, ALU.add, apply_absolute_value=True))
            dve.wait_ge(s["pe_setup"], 1)
            link(V.tensor_reduce(absrow[0:1, 1:2], banks[7][0:1, 0:S], AX_X, ALU.max))
            dve.wait_ge(s["pe_setup"], 2)
            link(V.tensor_copy(absrow[:, 2:3], banks[7][0:S, 0:1]))
            link(V.tensor_scalar(mask[:], sm("pow"), absrow[:, 2:3], None, ALU.is_lt))
            link(V.tensor_scalar(pick[:], mask[:], -1.0, 1.0, ALU.mult, ALU.add))
            link(V.tensor_tensor(pick[:], pick[:], sm("inv"), ALU.add))
            link(V.tensor_reduce(absrow[:, 3:4], pick[:], AX_X, ALU.min))
            link(V.tensor_scalar(absrow[:, 4:5], absrow[:, 3:4], 1.0, None, ALU.min))
            link(V.tensor_scalar(As[:].rearrange("p a b -> p (a b)"), As[:].rearrange("p a b -> p (a b)"),
                                 absrow[:, 4:5], None, ALU.mult))
            link(V.tensor_copy(XX[:, 0, :], ident[0:S, 0:S]))
            assert done[0] == SETUP_SERIES
            dve.wait_ge(s["halo_in"], 16 * 4 * B)
            row_stats(0, xc)
            for n in range(TERMS, 0, -1):
                dve.wait_ge(s["pe_setup"], 3 + TERMS - n)
                link(V.scalar_tensor_tensor(out=XX[:, 0, :], in0=banks[7][0:S, 0:S], scalar=1.0 / n,
                                            in1=ident[0:S, 0:S], op0=ALU.mult, op1=ALU.add))
            dve.wait_ge(s["xa_in"], 16 * B)
            row_stats(1, xa)
            dve.wait_ge(s["pe_setup"], 3 + TERMS)
            link(V.tensor_copy(XX[:, 1, :], banks[7][0:S, 0:S]))
            for n in range(SQUARINGS):
                if n == SQUARINGS - 7:
                    dve.wait_ge(s["y_done"], KH)
                    for k in range(KH):
                        V.memset(halo[:, k, :, 0, 0], 0.0)
                        ins = V.memset(halo[:, k, :, 1, NC - 1], 0.0)
                    ins.then_inc(s["halo_zeroed"], 1)
                dve.wait_ge(s["pe_setup"], 4 + TERMS + n)
                link(V.copy_predicated(XX[:].rearrange("p a b -> p (a b)"),
                                       mask[:, n:n + 1].bitcast(I32).to_broadcast([S, 2 * S]),
                                       banks[7][0:S, 0:2 * S]))
            link(V.tensor_reduce(absrow[:, 5:6], XX[:, 0, :], AX_X, ALU.add))
            link(V.tensor_scalar(absrow[:, 6:7], absrow[:, 5:6], -1.0 / S, None, ALU.mult))
            link(V.tensor_scalar(AC[:], XX[:, 0, :], absrow[:, 6:7], None, ALU.add))
            link(V.tensor_scalar(M[:], AC[:], sm("st_g"), None, ALU.mult))
            link(V.tensor_scalar(st_b_wide[:], st_b_wide[:], sm("st_b"), None, ALU.mult))
            link(V.tensor_reduce(absrow[0:1, 7:8], Bb[:], AX_X, ALU.add))
            link(V.tensor_scalar(absrow[0:1, 7:8], absrow[0:1, 7:8], -1.0 / S, None, ALU.mult))
            link(V.tensor_scalar(Bb[:], Bb[:], absrow[0:1, 7:8], None, ALU.add))
            dve.wait_ge(s["weights_in"], 16 * 7)
            link(V.tensor_reduce(btmp[:], BT[:], AX_X, ALU.add))
            link(V.tensor_scalar(btmp[:], btmp[:], -1.0 / S, None, ALU.mult))
            link(V.tensor_tensor(BT[:], BT[:], btmp[:].unsqueeze(2).to_broadcast([P, KH, S]), ALU.add))
            assert done[0] == SETUP_M
            dve.wait_ge(s["pe_setup"], SQ_END + 1)
            link(V.tensor_copy(dbias[:], banks[7][0:S, 0:1]))
            for k in range(KH):
                dve.wait_ge(s["wprime_mm"], k + 1)
                V.tensor_tensor(WT[:, k, :], WT[:, k, :], wbank[k][:], ALU.add).then_inc(s["wprime_done"], 1)

            def left_tap(c, k):
                wait_for(dve, "t1_done", KH, c, k + 1)
                if k == 0:
                    wait_for(dve, "halo_y", 1, c, 1)
                bank = cbank[k % 2][:].rearrange("p (b t) -> p b t", b=B)
                V.scalar_tensor_tensor(out=bank, in0=y[:, k, :, 0:CT], scalar=v_("conv_w0", k), in1=bank,
                                       op0=ALU.mult, op1=ALU.add).then_inc(s["conv_half"], 1)

            def right_tap(c, k, p):
                wait_for(dve, "conv_half", KH, c, k + 1)
                bank = cbank[k % 2][:].rearrange("p (b t) -> p b t", b=B)
                V.scalar_tensor_tensor(out=xnorm[p][:, k, :].rearrange("p (b t) -> p b t", b=B),
                                       in0=y[:, k, :, 2:CT + 2], scalar=v_("conv_w2", k), in1=bank,
                                       op0=ALU.mult, op1=ALU.add).then_inc(s["xnorm_done"], 1)

            def gated_x(c, m, p):
                wait_for(dve, "igs_done", KH, c, m + 1)
                if m == 0:
                    wait_for(dve, "b_mm", 1, c, 0)
                    wait_for(dve, "xnorm_done", KH, c, KH)
                V.tensor_tensor(xg[:, m, :], mbank["ig", m][:], xnorm[p][:, m, :],
                                ALU.mult).then_inc(s["xg_done"], 1)

            def silu(c, m, p):
                wait_for(dve, "sigf_done", KH, c, m + 1)
                V.scalar_tensor_tensor(out=G[p][:, m, :], in0=mbank["ffn", m][:], scalar=v_("ffn_b", m),
                                       in1=sigf[:, m % 2, :], op0=ALU.add, op1=ALU.mult
                                       ).then_inc(s["silu_done"], 1)

            def whole_gate(c, m, p):
                wait_for(dve, "gates_done", KH, c, m + 1)
                wait_for(dve, "silu_done", KH, c, m + 1)
                V.tensor_tensor(G[p][:, m, :], mbank["gate", m][:], G[p][:, m, :],
                                ALU.mult).then_inc(s["g_done"], 1)

            def state_times_c(c, p):
                wait_for(dve, "sn_done", 1, c, 1)
                wait_for(dve, "cT_done", 1, c, 1)
                wait_for(dve, "ssm_mm", KH, c, 0)
                V.tensor_tensor(ys[:], tbank["wr", 0][0:S, :], cT[p][:], ALU.mult).then_inc(s["ys_done"], 1)

            def gated_ssm(c, m, p):
                wait_for(dve, "ssm_mm", KH, c, m + 1)
                if m == 0:
                    wait_for(dve, "g_done", KH, c, KH)
                    wait_for(dve, "ofill", NJ, c, 0)
                V.scalar_tensor_tensor(out=sgT[:, m, :], in0=mbank["ssm", m][:], scalar=v_("D_b", m),
                                       in1=G[p][:, m, :], op0=ALU.add, op1=ALU.mult
                                       ).then_inc(s["sg_done"], 1)

            def add_x(c, j):
                wait_for(dve, "ofill", NJ, c, j + 1)
                wait_for(dve, OUT[j % 2], 8 * B, c, 16 * BJ * (j // 2))
                if j == 0:
                    wait_for(dve, "xc_in", 16 * B, c, 16 * B)
                V.tensor_tensor(o[:, j % 2, :], tbank["o", j][:], xc[:, j, :],
                                ALU.add).then_inc(s["o_done"], 1)

            def step(i, p, t):
                if t == 0:
                    wait_for(dve, "d_in", 16 * B, i, 16 * B)
                wait_for(dve, "p_ready", CT, i, t + 1)
                wait_for(dve, "r_ready", CT, i, t)
                w = dw[p][0:B, t, :]
                V.scalar_tensor_tensor(out=w, in0=scanP[0:B, 0:S], scalar=r[:], in1=w,
                                       op0=ALU.mult, op1=ALU.add).then_inc(s["w_ready"], 1)
                wait_for(dve, "w_ready", CT, i, t + 1)
                V.tensor_tensor_reduce(wq[:], w, w, 1.0 / S, EPS, ALU.mult, ALU.add,
                                       q[:]).then_inc(s["q_ready"], 1)
                V.transpose(wT[:], dw[p][:, t, :]).then_inc(s["wT_ready"], 1)

            for k in range(KH):
                left_tap(0, k)
                right_tap(0, k, 0)
            for m in range(KH):
                gated_x(0, m, 0)

            def iteration(i, p, parts):
                A, F, C = ("A" in parts), ("F" in parts), ("C" in parts)
                for t in range(CT):
                    if F:
                        step(i, p, t)
                    if A:
                        if t in V_STATS:
                            bn_stats(i + 2, t)
                        if t == V_AGGR:
                            aggregate(i + 2)
                        if t in V_CONV:
                            k, second = divmod(V_CONV.index(t), 2)
                            if second:
                                right_tap(i + 1, k, 1 - p)
                            else:
                                left_tap(i + 1, k)
                        if t in V_XG:
                            gated_x(i + 1, V_XG.index(t), 1 - p)
                    if F:
                        if t in V_SILU:
                            silu(i, V_SILU.index(t), p)
                        if t in V_G:
                            whole_gate(i, V_G.index(t), p)
                    if C:
                        if t == V_YS:
                            state_times_c(i - 1, 1 - p)
                        if t in V_SG:
                            gated_ssm(i - 1, V_SG.index(t), 1 - p)
                        if t in V_ADD:
                            add_x(i - 1, V_ADD.index(t))

            iteration(0, 0, "AF")
            iteration(1, 1, "AFC")
            with dve.Fori(1, NC // 2 - 1) as pair:
                i = dve.snap(2 * pair)
                iteration(i, 0, "AFC")
                iteration(i + 1, 1, "AFC")
            iteration(NC - 2, 0, "AFC")
            iteration(NC - 1, 1, "FC")
            iteration(NC, 0, "C")

        @block.tensor
        def _(pe):
            mm = nc.tensor.matmul
            tp = nc.tensor.transpose

            def fill_z(c, k, i, middle):
                wait_for(pe, "z_done", NJ, c + 1, NJ)
                wait_bank(pe, T_USERS, "z", k, i, middle)
                for j in range(NJ):
                    ins = tp(tbank["z", k][:, P * j:P * j + P], z[:, j, P * k:P * k + P], ident[:])
                ins.then_inc(s["zfill"], 1)

            def fill_x(c, k, i, middle):
                wait_for(pe, "xn_done", NJ, c, NJ)
                wait_bank(pe, T_USERS, "x", k, i, middle)
                for j in range(NJ):
                    ins = tp(tbank["x", k][:, P * j:P * j + P], z[:, j, P * k:P * k + P], ident[:])
                ins.then_inc(s["xfill"], 1)

            def fill_w(c, j, i, middle):
                if j == 0:
                    wait_for(pe, "wr_done", NJ, c, NJ)
                    wait_bank(pe, T_USERS, "wr", 0, i, middle)
                    hold(pe)
                ins = tp(tbank["wr", 0][0:S, P * j:P * j + P], wr[:, j, :], ident[:])
                if j == NJ - 1:
                    ins.then_inc(s["wrfill"], 1)

            def fill_o(c, j, m, i, middle):
                if m == 0:
                    wait_for(pe, "sg_done", KH, c, KH)
                    wait_bank(pe, T_USERS, "o", j, i, middle)
                ins = tp(tbank["o", j][:, P * m:P * m + P], sgT[:, m, P * j:P * j + P], ident[:])
                if m == KH - 1:
                    ins.then_inc(s["ofill"], 1)

            def fill_d(c, i, middle):
                wait_for(pe, "dT_done", 1, c, 1)
                wait_bank(pe, T_USERS, "d", 0, i, middle)
                hold(pe)
                for j in range(NJ):
                    ins = tp(tbank["d", 0][:, S * j:S * j + S], dT[:, P * j:P * j + P], ident[0:S, 0:S])
                ins.then_inc(s["dfill"], 1)

            def ffn(c, m, k, i, middle):
                if k == 0:
                    wait_for(pe, "xnT_done", KH, c, KH)
                    wait_bank(pe, M_USERS, "ffn", m, i, middle)
                ins = mm(mbank["ffn", m][:], WT[:, k, P * m:P * m + P], xnT[:, k, :],
                         start=(k == 0), stop=(k == KH - 1))
                if k == KH - 1:
                    ins.then_inc(s["ffn_mm"], 1)

            def gate(c, m, k, p, i, middle):
                if k == 0:
                    wait_bank(pe, M_USERS, "gate", m, i, middle)
                ins = mm(mbank["gate", m][:], gateT[:, k, P * m:P * m + P], xnorm[p][:, k, :],
                         start=(k == 0), stop=(k == KH - 1))
                if k == KH - 1:
                    ins.then_inc(s["gate_mm"], 1)

            def in_gate(c, m, k, p, i, middle):
                if k == 0:
                    wait_for(pe, "xnorm_done", KH, c, KH)
                    wait_bank(pe, M_USERS, "ig", m, i, middle)
                ins = mm(mbank["ig", m][:], gateT[:, k, H + P * m:H + P * m + P], xnorm[p][:, k, :],
                         start=(k == 0), stop=(k == KH - 1))
                if k == KH - 1:
                    ins.then_inc(s["ig_mm"], 1)

            def b_proj(c, k, i, middle):
                if k == 0:
                    wait_bank(pe, M_USERS, "b", 0, i, middle)
                wait_for(pe, "xg_done", KH, c, k + 1)
                ins = mm(mbank["b", 0][0:S, :], BT[:, k, :], xg[:, k, :], start=(k == 0), stop=(k == KH - 1))
                if k == KH - 1:
                    ins.then_inc(s["b_mm"], 1)

            def c_proj(c, k, p, i, middle):
                if k == 0:
                    wait_bank(pe, M_USERS, "c", 0, i, middle)
                ins = mm(mbank["c", 0][0:S, :], CwT[:, k, :], xnorm[p][:, k, :],
                         start=(k == 0), stop=(k == KH - 1))
                if k == KH - 1:
                    ins.then_inc(s["c_mm"], 1)

            def ssm(c, m, i, middle):
                if m == 0:
                    wait_for(pe, "ys_done", 1, c, 1)
                wait_bank(pe, M_USERS, "ssm", m, i, middle)
                mm(mbank["ssm", m][:], DT[:, P * m:P * m + P], ys[:],
                   start=True, stop=True).then_inc(s["ssm_mm"], 1)

            def step(i, t):
                wait_for(pe, "wT_ready", CT, i, t + 1)
                hold(pe)
                mm(scanP[0:B, 0:S], wT[:, 0:B], M2[:, 0, :], start=True, stop=False)
                mm(scanP[0:B, 0:S], wT[:, 32:32 + B], M2[:, 1, :], start=False, stop=True
                   ).then_inc(s["p_ready"], 1)

            pe.wait_ge(s["consts"], 16 * 4)
            pe.wait_ge(s["dve_setup"], SETUP_VEC + 2)
            tp(banks[7][0:1, 0:S], absrow[:, 0:1], ident[0:S, 0:S]).then_inc(s["pe_setup"], 1)
            pe.wait_ge(s["dve_setup"], SETUP_VEC + 3)
            mm(banks[7][0:S, 0:1], ones[0:1, 0:S], absrow[0:1, 1:2], start=True, stop=True
               ).then_inc(s["pe_setup"], 1)
            for n in range(TERMS):
                pe.wait_ge(s["dve_setup"], SETUP_SERIES + n)
                mm(banks[7][0:S, 0:S], As[:, 1, :], XX[:, 0, :], start=True, stop=True
                   ).then_inc(s["pe_setup"], 1)
            pe.wait_ge(s["dve_setup"], SETUP_SERIES + TERMS)
            tp(banks[7][0:S, 0:S], XX[:, 0, :], ident[0:S, 0:S]).then_inc(s["pe_setup"], 1)
            for k in range(KH):
                fill_z(-1, k, -2, False)
            for n in range(SQUARINGS):
                if n == SQUARINGS - 6:
                    for k in range(KH):
                        fill_z(0, k, -1, False)
                pe.wait_ge(s["dve_setup"], SETUP_SERIES + TERMS + 1 + n)
                mm(banks[7][0:S, 0:S], XX[:, 1, :], XX[:, 0, :], start=True, stop=True)
                mm(banks[7][0:S, S:2 * S], XX[:, 0, :], XX[:, 1, :], start=True, stop=True
                   ).then_inc(s["pe_setup"], 1)
            pe.wait_ge(s["dve_setup"], SETUP_M)
            mm(banks[7][0:S, 0:1], AC[:], sm("st_b"), start=True, stop=False)
            mm(banks[7][0:S, 0:1], Bb[:], ones[0:1, 0:1], start=False, stop=True).then_inc(s["pe_setup"], 1)
            mm(scanP[0:B, 0:S], st_b_wide[:, 0:B], AC[:], start=True, stop=True).then_inc(s["p_ready"], 1)
            pe.wait_ge(s["dve_setup"], SETUP_M + 1)
            for k in range(KH):
                if k == KH - 1:
                    pe.wait_ge(s["wprime_done"], 1)
                mm(wbank[k][:], VT[:, P * k:P * k + P], CrT[:], start=True, stop=True
                   ).then_inc(s["wprime_mm"], 1)
            pe.wait_ge(s["m2_in"], 32)
            for k in range(KH):
                fill_x(0, k, -1, False)
            pe.wait_ge(s["wprime_done"], KH)
            for m in range(KH):
                for k in range(KH):
                    in_gate(0, m, k, 0, -1, False)
            for k in range(KH):
                b_proj(0, k, -1, False)
            fill_d(0, -1, False)
            for k in range(KH):
                c_proj(0, k, 0, -1, False)

            def iteration(i, p, parts, middle):
                A, F, C = ("A" in parts), ("F" in parts), ("C" in parts)
                for t in range(CT):
                    if F:
                        step(i, t)
                        if t in PE_FFN:
                            ffn(i, *divmod(PE_FFN.index(t), KH), i, middle)
                    if C:
                        if t in PE_W:
                            fill_w(i - 1, PE_W.index(t), i, middle)
                        if t in PE_SSM:
                            ssm(i - 1, PE_SSM.index(t), i, middle)
                    if A:
                        for k in range(KH):
                            if PE_Z[k] == t:
                                fill_z(i + 1, k, i, middle)
                            if PE_X[k] == t:
                                fill_x(i + 1, k, i, middle)
                    if F and t in PE_GATE:
                        m, k = divmod(PE_GATE.index(t), KH)
                        gate(i, m, k, p, i, middle)
                    if C and t in PE_O:
                        fill_o(i - 1, *divmod(PE_O.index(t), KH), i, middle)
                    if A:
                        if t in PE_IG:
                            in_gate(i + 1, *divmod(PE_IG.index(t), KH), 1 - p, i, middle)
                        if t in PE_B:
                            b_proj(i + 1, PE_B.index(t), i, middle)
                        if t == PE_D:
                            fill_d(i + 1, i, middle)
                        if t in PE_C:
                            c_proj(i + 1, PE_C.index(t), 1 - p, i, middle)

            iteration(0, 0, "AF", False)
            iteration(1, 1, "AFC", False)
            with pe.Fori(1, NC // 2 - 1) as pair:
                i = pe.snap(2 * pair)
                iteration(i, 0, "AFC", True)
                iteration(i + 1, 1, "AFC", True)
            iteration(NC - 2, 0, "AFC", False)
            iteration(NC - 1, 1, "FC", False)
            iteration(NC, 0, "C", False)


LN_OPS = 12
SETUP_VEC = 1
SETUP_SERIES = SETUP_VEC + 11
SETUP_M = SETUP_SERIES + TERMS + 1 + SQUARINGS + 11
SQ_END = 3 + TERMS + SQUARINGS


def kernel(**inputs):
    import concourse.bacc as _bacc
    from concourse.bass_utils import run_bass_kernel_spmd as _run

    a = {k: np.asarray(v) for k, v in inputs.items()}
    at = {k[len("L0_attn_"):]: v for k, v in a.items() if k.startswith("L0_attn_")}
    blocks = lambda v: v.reshape(KH, P).T
    conv = at["conv_w"].reshape(H, 3)
    parts = {"ln_g": at["ln_in_g"], "ln_b": at["ln_in_b"], "conv_w0": conv[:, 0], "conv_w1": conv[:, 1],
             "conv_w2": conv[:, 2], "conv_b": at["conv_b"], "gate_b": at["gate_b"][:H],
             "in_gate_b": at["gate_b"][H:], "ffn_b": a["L0_ffn_b"], "D_b": at["D_b"]}
    vec = np.stack([blocks(parts[n]) for n in VEC], axis=1)
    powers = np.float32(2.0) ** np.arange(SQUARINGS, dtype=np.float32)
    halves = np.float32(0.5) ** np.arange(1, SQUARINGS + 1, dtype=np.float32)
    small = np.concatenate([
        at["A"], at["A"].T, at["ln_st_g"][:, None], at["ln_st_b"][:, None], at["C_b"][:, None],
        np.broadcast_to(at["dt_A"].reshape(1, 1), (S, 1)),
        np.broadcast_to(powers, (S, SQUARINGS)), np.broadcast_to(halves, (S, SQUARINGS))], axis=1)
    arrays = {
        "x": at["x"], "ident": np.eye(P, dtype=np.float32), "gateT": at["gate_w"].T, "WT": a["L0_ffn_W"].T,
        "VT": a["L0_ffn_V_r"].T, "CrT": a["L0_ffn_C"].T, "BT": at["B_w"].T, "CwT": at["C_w"].T,
        "DT": at["D_w"].T, "vec": vec, "small": small, "Bb": at["B_b"].reshape(1, S),
    }
    nc = _bacc.Bacc("TRN2", target_bir_lowering=False, num_devices=1)
    held, args = {}, []
    for name, v in arrays.items():
        v = np.ascontiguousarray(v)
        held[f"in_{name}"] = v
        args.append(nc.dram_tensor(f"in_{name}", v.shape, mybir.dt.from_np(v.dtype), kind="ExternalInput").ap())
    out = nc.dram_tensor("out_0", (B, T, H), F32, kind="ExternalOutput").ap()
    build(nc, *args, out)
    r = _run(nc, [held], core_ids=[0])
    return r.results[0]["out_0"]
```

```python
from contextlib import ExitStack

import numpy as np

import concourse.bass as bass
from concourse import mybir

ALU = mybir.AluOpType
ACT = mybir.ActivationFunctionType
F32 = mybir.dt.float32
I32 = mybir.dt.int32
AX_X = mybir.AxisListType.X

P = 128
B = 8
T = 2048
H = 512
S = 64
R = 32
KH = H // P
CT = 64
NC = T // CT
TOK = B * CT
NJ = TOK // P
BJ = B // NJ
EPS = 1e-5
SQUARINGS = 20
TERMS = 12

OUT = ["out_even", "out_odd"]

VEC = ["ln_g", "ln_b", "conv_w0", "conv_w1", "conv_w2", "conv_b", "gate_b", "in_gate_b", "ffn_b", "D_b"]
SMALL = {"A": (0, S), "AT": (S, S), "st_g": (2 * S, 1), "st_b": (2 * S + 1, 1), "C_b": (2 * S + 2, 1),
         "dt": (2 * S + 3, 1), "pow": (2 * S + 4, SQUARINGS), "inv": (2 * S + 4 + SQUARINGS, SQUARINGS)}
SMALL_W = 2 * S + 4 + 2 * SQUARINGS

T_USERS = [("z", k, "A") for k in range(KH)] + [("wr", 0, "C")] + [("x", k, "A") for k in range(KH)] \
    + [("o", j, "C") for j in range(NJ)] + [("d", 0, "A")]
M_USERS = [("ffn", m, "F") for m in range(KH)] + [("ssm", m, "C") for m in range(KH)] \
    + [("ig", m, "A") for m in range(KH)] + [("b", 0, "A")] + [("gate", m, "F") for m in range(KH)] \
    + [("c", 0, "A")]

PE_Z = (3, 3, 6, 6)
PE_FFN = (0, 1, 2, 4) + (5, 7, 8, 9) + tuple(range(10, 18))
PE_W = range(11, 15)
PE_X = (18, 18, 21, 21)
PE_SSM = (19, 20, 22, 23)
PE_IG = range(24, 40)
PE_O = range(27, 43)
PE_B = range(40, 44)
PE_GATE = range(44, 60)
PE_D = range(46, 50)
PE_C = range(60, 64)
V_CONV = (7, 8, 9, 10, 12, 13, 14, 15)
V_SILU = (11, 16, 18, 20)
V_YS = 17
V_SG = (21, 22, 24, 25)
V_STATS = (26, 27, 28, 30)
V_AGGR = 31
V_XG = (29, 33, 37, 41)
V_ADD = (32, 36, 40, 44)
V_G = (49, 53, 57, 61)
POOL_RS = (7, 8, 9)
POOL_LN = (36, 36, 37, 38, 39, 40, 41, 42, 43, 44, 44, 45)


def build(nc, x, ident_d, gateT_d, WT_d, VT_d, CrT_d, BT_d, CwT_d, DT_d, vec_d, small_d, Bb_d, out):
    with ExitStack() as ctx:
        def sb(name, shape, dt=F32):
            return ctx.enter_context(nc.sbuf_tensor(name, shape, dt))

        def sem(name):
            return ctx.enter_context(nc.semaphore(name))

        ident = sb("ident", [P, P])
        gateT = sb("gateT", [P, KH, 2 * H])
        WT = sb("WT", [P, KH, H])
        VT = sb("VT", [R, H])
        CrT = sb("CrT", [R, H])
        BT = sb("BT", [P, KH, S])
        CwT = sb("CwT", [P, KH, S])
        DT = sb("DT", [S, H])
        vec = sb("vec", [P, len(VEC), KH])
        small = sb("small", [S, SMALL_W])
        Bb = sb("Bb", [1, S])
        ones = sb("ones", [1, P])
        minus_half = sb("minus_half", [P, NJ])
        dbias = sb("dbias", [S, 1])
        btmp = sb("btmp", [P, KH])
        As = sb("As", [S, 2, S])
        absrow = sb("absrow", [S, 8])
        XX = sb("XX", [S, 2, S])
        mask = sb("mask", [S, SQUARINGS])
        pick = sb("pick", [S, SQUARINGS])
        AC = sb("AC", [S, S])
        M = sb("M", [S, S])
        M2 = sb("M2", [32, 2, S])
        st_b_wide = sb("st_b_wide", [S, P])
        xa = sb("xa", [P, NJ, H])
        xc = sb("xc", [P, NJ, H])
        stats = sb("stats", [P, NJ, 6])
        mv = sb("mv", [P, NJ, 2])
        ln = sb("ln", [P, 8, NJ])
        z = sb("z", [P, NJ, H])
        y = sb("y", [P, KH, B, CT + 2])
        halo = sb("halo", [P, KH, B, 2, NC])
        xnT = sb("xnT", [P, KH, TOK])
        xnorm = [sb(f"xnorm{p}", [P, KH, TOK]) for p in range(2)]
        xg = sb("xg", [P, KH, TOK])
        sigf = sb("sigf", [P, 2, TOK])
        G = [sb(f"G{p}", [P, KH, TOK]) for p in range(2)]
        cT = [sb(f"cT{p}", [S, TOK]) for p in range(2)]
        dT = sb("dT", [S, TOK])
        dtok = sb("dtok", [P, NJ, S])
        dw = [sb(f"dw{p}", [32, CT, S]) for p in range(2)]
        wtok = sb("wtok", [P, NJ, S])
        wsq = sb("wsq", [P, NJ, S])
        ssq = sb("ssq", [P, 3, NJ])
        wr = sb("wr", [P, NJ, S])
        ys = sb("ys", [S, TOK])
        sgT = sb("sgT", [P, KH, TOK])
        o = sb("o", [P, 2, H])
        wT = sb("wT", [32, S])
        wq = sb("wq", [B, S])
        q = sb("q", [B, 1])
        r = sb("r", [B, 1])

        banks = [ctx.enter_context(nc.psum_tensor(f"bank{n}", [P, TOK], F32)) for n in range(8)]
        scanP = banks[0]
        tbank = {}
        for n, (what, k, _) in enumerate(T_USERS):
            tbank[what, k] = banks[1 + n % 2]
        mbank = {}
        for n, (what, k, _) in enumerate(M_USERS):
            mbank[what, k] = banks[[3, 4, 7][n % 3]]
        cbank = [banks[5], banks[6]]
        wbank = [banks[3], banks[4], banks[7], banks[3]]

        names = """held consts weights_in halo_in xa_in xc_in d_in w_in out_even out_odd dve_cleared pool_cleared pe_setup dve_setup halo_zeroed xc_cleared m2_in wprime_mm wprime_done
            p_ready r_ready w_ready q_ready wT_ready
            stats_done mv_done ln_done z_done zfill y_done halo_y t1_done conv_half xnorm_done xn_done xfill xnT_done
            ig_mm igs_done xg_done b_mm dT_done dfill dtok_done c_mm cT_done
            ffn_mm sigf_done silu_done gate_mm gates_done g_done
            ssq_done rs_done wr_done wrfill sn_done ys_done ssm_mm sg_done ofill o_done""".split()
        s = {n: sem(n) for n in names}

        vcol = {n: i for i, n in enumerate(VEC)}

        def v_(name, k):
            return vec[:, vcol[name], k:k + 1]

        def sm(name):
            a, w = SMALL[name]
            return small[:, a:a + w]

        def released(user, i):
            what, k = user
            return {
                "z": lambda: ("y_done", KH, i + 2, k + 1),
                "x": lambda: ("xnT_done", KH, i + 1, k + 1),
                "wr": lambda: ("ys_done", 1, i, 0),
                "o": lambda: ("o_done", NJ, i - 1, k + 1),
                "ffn": lambda: ("silu_done", KH, i, k + 1),
                "gate": lambda: ("g_done", KH, i, k + 1),
                "ssm": lambda: ("sg_done", KH, i - 1, k + 1),
                "ig": lambda: ("xg_done", KH, i + 1, k + 1),
                "b": lambda: ("dT_done", 1, i + 1, 1),
                "d": lambda: ("dtok_done", 1, i + 1, 1),
                "c": lambda: ("cT_done", 1, i + 1, 1),
            }[what]()

        def parts_of(i, middle):
            if middle:
                return "AFC"
            return {-2: "z", -1: "A", 0: "AF", NC - 1: "FC", NC: "C"}.get(i, "AFC" if 0 < i < NC else "")

        def wait_for(eng, name, per, n, k):
            v = n * per + k
            if isinstance(v, int) and v <= 0:
                return
            eng.wait_ge(s[name], v)

        def hold(eng):
            eng.sem_inc(s["held"], 1)

        def wait_bank(eng, users, what, k, i, middle):
            n = [u[:2] for u in users].index((what, k))
            size = 2 if users is T_USERS else 3
            back, at = 0, n
            while back < 4:
                at -= 1
                if at < 0:
                    at, back = len(users) - 1, back + 1
                same = at % size == n % size
                parts = parts_of(i if middle else i - back, middle)
                here = users[at][2] in parts or (parts == "z" and users[at][0] == "z")
                if same and here:
                    wait_for(eng, *released(users[at][:2], i - back))
                    return

        block = ctx.enter_context(nc.Block())

        @block.sync
        def _(sp):
            def load_x(dst, c, name):
                for j in range(NJ):
                    sp.dma_start(dst[:, j, :],
                                 x[BJ * j:BJ * (j + 1), bass.ds(c * CT, CT), :]).then_inc(s[name], 16)

            for dst, src in [(small[:], small_d), (ident[:], ident_d), (vec[:], vec_d), (Bb[:], Bb_d)]:
                sp.dma_start(dst, src).then_inc(s["consts"], 16)
            load_x(xa, 0, "xa_in")
            sp.wait_ge(s["xc_cleared"], 1)
            for b in range(B):
                p0 = CT * (b % BJ)
                for a, e in ((1, NC // 2 + 1), (NC // 2 + 1, NC)):
                    sp.dma_start(xc[p0 + a:p0 + e, b // BJ, :],
                                 x[b, CT * a - 1:CT * (e - 1):CT, :]).then_inc(s["halo_in"], 16)
                for a, e in ((0, NC // 2), (NC // 2, NC - 1)):
                    sp.dma_start(xc[p0 + NC + a:p0 + NC + e, b // BJ, :],
                                 x[b, CT * (a + 1):CT * e + 1:CT, :]).then_inc(s["halo_in"], 16)
            for dst, src in [(BT[:], BT_d.rearrange("(k p) n -> p k n", p=P)), (VT[:], VT_d), (CrT[:], CrT_d),
                             (WT[:], WT_d.rearrange("(k p) n -> p k n", p=P)),
                             (gateT[:], gateT_d.rearrange("(k p) n -> p k n", p=P)),
                             (CwT[:], CwT_d.rearrange("(k p) n -> p k n", p=P)), (DT[:], DT_d)]:
                sp.dma_start(dst, src).then_inc(s["weights_in"], 16)

            def send_d(c, p):
                if isinstance(c, int) and c == 0:
                    sp.wait_ge(s["pool_cleared"], 2)
                wait_for(sp, "dtok_done", 1, c, 1)
                hold(sp)
                wait_for(sp, "w_in", 16 * NJ, c - 1, 0)
                for j in range(NJ):
                    sp.dma_start(dw[p][BJ * j:BJ * (j + 1), :, :], dtok[:, j, :]).then_inc(s["d_in"], 16)

            def send_w(c, p):
                wait_for(sp, "w_ready", CT, c, CT)
                hold(sp)
                wait_for(sp, "wr_done", NJ, c, 0)
                for j in range(NJ):
                    sp.dma_start(wtok[:, j, :], dw[p][BJ * j:BJ * (j + 1), :, :]).then_inc(s["w_in"], 16)

            def prefetch_xa(c):
                wait_for(sp, "xn_done", NJ, c, 0)
                hold(sp)
                load_x(xa, c, "xa_in")

            def send_out(c, j):
                wait_for(sp, "o_done", NJ, c, j + 1)
                hold(sp)
                sp.dma_start(out[BJ * j:BJ * (j + 1), bass.ds(c * CT, CT), :],
                             o[:, j % 2, :]).then_inc(s[OUT[j % 2]], 16)

            prefetch_xa(1)
            sp.wait_ge(s["dve_setup"], SETUP_M - 7)
            for h in range(2):
                sp.dma_start(M2[:, h, :], M[32 * h:32 * h + 32, :]).then_inc(s["m2_in"], 16)
            send_d(0, 0)

            def iteration(i, p, parts, middle):
                if "C" in parts:
                    send_w(i - 1, 1 - p)
                if "A" in parts and (middle or i + 2 < NC):
                    prefetch_xa(i + 2)
                if "C" in parts:
                    for j in range(NJ):
                        send_out(i - 1, j)
                if "F" in parts:
                    wait_for(sp, "z_done", NJ, i, NJ)
                    hold(sp)
                    wait_for(sp, "o_done", NJ, i, 0)
                    hold(sp)
                    load_x(xc, i, "xc_in")
                if "A" in parts:
                    send_d(i + 1, 1 - p)

            iteration(0, 0, "ASF", False)
            iteration(1, 1, "ASFC", False)
            with sp.Fori(1, NC // 2 - 1) as pair:
                i = sp.snap(2 * pair)
                iteration(i, 0, "ASFC", True)
                iteration(i + 1, 1, "ASFC", True)
            iteration(NC - 2, 0, "AFC", False)
            iteration(NC - 1, 1, "FC", False)
            iteration(NC, 0, "C", False)
            for name in OUT:
                sp.wait_ge(s[name], 8 * NJ * NC)

        @block.gpsimd
        def _(pool):
            nc.gpsimd.memset(minus_half[:], -0.5).then_inc(s["pool_cleared"], 1)
            nc.gpsimd.memset(dw[0][:], 0.0)
            nc.gpsimd.memset(dw[1][:], 0.0).then_inc(s["pool_cleared"], 1)
            pool.wait_ge(s["pool_cleared"], 2)
            pool.wait_ge(s["dve_cleared"], 1)

            def step(i, t):
                wait_for(pool, "q_ready", CT, i, t + 1)
                nc.gpsimd.tensor_tensor(r[:], q[:], minus_half[0:B, 0:1], ALU.pow).then_inc(s["r_ready"], 1)

            def ln_op(n, k):
                mean, var = mv[:, :, 0], mv[:, :, 1]
                nm, a, r1, v2, r2, rr, bx, bz = (ln[:, a, :] for a in range(8))
                if k == 0:
                    wait_for(pool, "mv_done", NJ, n, NJ)
                    wait_for(pool, "xn_done", NJ, n - 1, 0)
                    wait_for(pool, "z_done", NJ, n, 0)
                else:
                    wait_for(pool, "ln_done", LN_OPS, n, k)
                hold(pool)
                g = nc.gpsimd
                ins = [
                    lambda: g.tensor_scalar(nm, mean, -1.0, None, ALU.mult),
                    lambda: g.tensor_scalar(a, var, EPS, None, ALU.add),
                    lambda: g.tensor_tensor(r1[:, 0:2], a[:, 0:2], minus_half[:, 0:2], ALU.pow),
                    lambda: g.tensor_tensor(r1[:, 2:4], a[:, 2:4], minus_half[:, 2:4], ALU.pow),
                    lambda: g.tensor_tensor(v2, var, r1, ALU.mult),
                    lambda: g.tensor_tensor(v2, v2, r1, ALU.mult),
                    lambda: g.tensor_scalar(a, v2, EPS, None, ALU.add),
                    lambda: g.tensor_tensor(r2[:, 0:2], a[:, 0:2], minus_half[:, 0:2], ALU.pow),
                    lambda: g.tensor_tensor(r2[:, 2:4], a[:, 2:4], minus_half[:, 2:4], ALU.pow),
                    lambda: g.tensor_tensor(rr, r1, r2, ALU.mult),
                    lambda: g.tensor_tensor(bx, nm, r1, ALU.mult),
                    lambda: g.tensor_tensor(bz, nm, rr, ALU.mult),
                ][k]()
                ins.then_inc(s["ln_done"], 1)

            def state_scale(c, k):
                if k == 0:
                    wait_for(pool, "ssq_done", NJ, c, NJ)
                    hold(pool)
                    nc.gpsimd.tensor_scalar(ssq[:, 1, :], ssq[:, 0, :], EPS, None,
                                            ALU.add).then_inc(s["rs_done"], 1)
                else:
                    wait_for(pool, "rs_done", 3, c, k)
                    wait_for(pool, "wr_done", NJ, c, 0)
                    half = slice(2 * k - 2, 2 * k)
                    nc.gpsimd.tensor_tensor(ssq[:, 2, half], ssq[:, 1, half], minus_half[:, half],
                                            ALU.pow).then_inc(s["rs_done"], 1)

            for n in range(3):
                for k in range(LN_OPS):
                    ln_op(n, k)

            def iteration(i, parts):
                for t in range(CT):
                    if "F" in parts:
                        step(i, t)
                    if "C" in parts and t in POOL_RS:
                        state_scale(i - 1, POOL_RS.index(t))
                    if "S" in parts:
                        for k in range(LN_OPS):
                            if POOL_LN[k] == t:
                                ln_op(i + 3, k)

            iteration(0, "ASF")
            iteration(1, "ASFC")
            with pool.Fori(1, NC // 2 - 1) as pair:
                i = pool.snap(2 * pair)
                iteration(i, "ASFC")
                iteration(i + 1, "ASFC")
            iteration(NC - 2, "AFC")
            iteration(NC - 1, "FC")
            iteration(NC, "C")

        @block.scalar
        def _(act):
            a_ = nc.scalar.activation

            def normalise_z(n, src=xa):
                wait_for(act, "ln_done", LN_OPS, n, LN_OPS)
                wait_for(act, "xfill", KH, n - 1, 0)
                for j in range(NJ):
                    a_(z[:, j, :], src[:, j, :], ACT.Identity, bias=ln[:, 7, j:j + 1],
                       scale=ln[:, 5, j:j + 1]).then_inc(s["z_done"], 1)

            def normalise_x(c, tiles):
                if tiles[0] == 0:
                    wait_for(act, "zfill", KH, c + 1, KH)
                for j in tiles:
                    a_(z[:, j, :], xa[:, j, :], ACT.Identity, bias=ln[:, 6, j:j + 1],
                       scale=ln[:, 2, j:j + 1]).then_inc(s["xn_done"], 1)

            def make_y(c, k):
                wait_for(act, "zfill", KH, c + 1, k + 1)
                wait_for(act, "xnorm_done", KH, c - 1, k + 1)
                a_(y[:, k, :, 1:CT + 1], tbank["z", k][:].rearrange("p (b t) -> p b t", b=B),
                   ACT.Identity, bias=v_("ln_b", k), scale=v_("ln_g", k)).then_inc(s["y_done"], 1)

            def copy_halo(c):
                wait_for(act, "xnorm_done", KH, c, 0)
                nc.scalar.copy(y[:, :, :, 0:CT + 2:CT + 1],
                               halo[:, :, :, :, bass.ds(c, 1)].rearrange("p k b s o -> p k b (s o)")
                               ).then_inc(s["halo_y"], 1)

            def centre_tap(c, k):
                wait_for(act, "y_done", KH, c + 1, k + 1)
                wait_for(act, "xnorm_done", KH, c, k - 1)
                a_(cbank[k % 2][:].rearrange("p (b t) -> p b t", b=B), y[:, k, :, 1:CT + 1],
                   ACT.Identity, bias=v_("conv_b", k), scale=v_("conv_w1", k)).then_inc(s["t1_done"], 1)

            def copy_xnT(c, k):
                wait_for(act, "xfill", KH, c, k + 1)
                wait_for(act, "ffn_mm", KH, c, 0)
                nc.scalar.copy(xnT[:, k, :], tbank["x", k][:]).then_inc(s["xnT_done"], 1)

            def input_gate(c, m):
                wait_for(act, "ig_mm", KH, c, m + 1)
                a_(mbank["ig", m][:], mbank["ig", m][:], ACT.Sigmoid,
                   bias=v_("in_gate_b", m)).then_inc(s["igs_done"], 1)

            def copy_c(c, p):
                wait_for(act, "c_mm", 1, c, 1)
                wait_for(act, "ys_done", 1, c - 1, 0)
                a_(cT[p][:], mbank["c", 0][0:S, :], ACT.Identity, bias=sm("C_b")).then_inc(s["cT_done"], 1)

            def copy_dT(c):
                wait_for(act, "b_mm", 1, c, 1)
                a_(dT[:], mbank["b", 0][0:S, :], ACT.Identity, bias=dbias[:]).then_inc(s["dT_done"], 1)

            def copy_dtok(c):
                wait_for(act, "dfill", 1, c, 1)
                wait_for(act, "d_in", 16 * NJ, c, 0)
                nc.scalar.copy(dtok[:].rearrange("p j e -> p (j e)"),
                               tbank["d", 0][:, 0:NJ * S]).then_inc(s["dtok_done"], 1)

            def ffn_sigmoid(c, m):
                wait_for(act, "ffn_mm", KH, c, m + 1)
                wait_for(act, "silu_done", KH, c, m - 1)
                a_(sigf[:, m % 2, :], mbank["ffn", m][:], ACT.Sigmoid,
                   bias=v_("ffn_b", m)).then_inc(s["sigf_done"], 1)

            def gate_sigmoid(c, m):
                wait_for(act, "gate_mm", KH, c, m + 1)
                a_(mbank["gate", m][:], mbank["gate", m][:], ACT.Sigmoid,
                   bias=v_("gate_b", m)).then_inc(s["gates_done"], 1)

            def state_squares(c):
                wait_for(act, "w_in", 16 * NJ, c, 16 * NJ)
                wait_for(act, "rs_done", 3, c, 0)
                for j in range(NJ):
                    a_(wsq[:, j, :], wtok[:, j, :], ACT.Square, scale=float(S) ** -0.5,
                       accum_out=ssq[:, 0, j:j + 1]).then_inc(s["ssq_done"], 1)

            def state_normalise(c):
                wait_for(act, "rs_done", 3, c, 3)
                wait_for(act, "wrfill", 1, c, 0)
                for j in range(NJ):
                    a_(wr[:, j, :], wtok[:, j, :], ACT.Copy,
                       scale=ssq[:, 2, j:j + 1]).then_inc(s["wr_done"], 1)

            def state_affine(c):
                wait_for(act, "wrfill", 1, c, 1)
                bank = tbank["wr", 0][0:S, :]
                a_(bank, bank, ACT.Identity, bias=sm("st_b"), scale=sm("st_g")).then_inc(s["sn_done"], 1)

            act.wait_ge(s["consts"], 16 * 4)
            act.wait_ge(s["dve_setup"], SETUP_VEC)
            normalise_z(0, xc)
            for k in range(KH):
                act.wait_ge(s["zfill"], k + 1)
                a_(halo[:, k].rearrange("p b s c -> p (b s c)"), tbank["z", k][:], ACT.Identity,
                   bias=v_("ln_b", k), scale=v_("ln_g", k)).then_inc(s["y_done"], 1)
            normalise_z(1)

            def first_taps(c):
                for k in range(2):
                    make_y(c, k)
                for k in range(2):
                    centre_tap(c, k)

            act.wait_ge(s["halo_zeroed"], 1)
            copy_halo(0)
            first_taps(0)
            for k in range(2, 4):
                make_y(0, k)
            normalise_x(0, (0, 1))
            centre_tap(0, 2)
            normalise_x(0, (2, 3))
            centre_tap(0, 3)
            for k in range(KH):
                copy_xnT(0, k)
            for m in range(KH):
                input_gate(0, m)
            act.wait_ge(s["dve_setup"], SETUP_M + 1)
            copy_dT(0)
            copy_dtok(0)
            copy_c(0, 0)

            def iteration(i, p, parts):
                A, F, C = ("A" in parts), ("F" in parts), ("C" in parts)
                if A:
                    normalise_z(i + 2)
                    copy_halo(i + 1)
                    first_taps(i + 1)
                if C:
                    state_squares(i - 1)
                if F:
                    ffn_sigmoid(i, 0)
                if A:
                    for k in range(2, 4):
                        make_y(i + 1, k)
                    normalise_x(i + 1, (0, 1))
                    centre_tap(i + 1, 2)
                if C:
                    state_normalise(i - 1)
                if A:
                    normalise_x(i + 1, (2, 3))
                    centre_tap(i + 1, 3)
                if F:
                    ffn_sigmoid(i, 1)
                    ffn_sigmoid(i, 2)
                if C:
                    state_affine(i - 1)
                if F:
                    ffn_sigmoid(i, 3)
                if A:
                    for k in range(KH):
                        copy_xnT(i + 1, k)
                    for m in range(KH):
                        input_gate(i + 1, m)
                    copy_dT(i + 1)
                if F:
                    gate_sigmoid(i, 0)
                if A:
                    copy_dtok(i + 1)
                if F:
                    for m in range(1, KH):
                        gate_sigmoid(i, m)
                if A:
                    copy_c(i + 1, 1 - p)

            iteration(0, 0, "ASF")
            iteration(1, 1, "ASFC")
            with act.Fori(1, NC // 2 - 1) as pair:
                i = act.snap(2 * pair)
                iteration(i, 0, "ASFC")
                iteration(i + 1, 1, "ASFC")
            iteration(NC - 2, 0, "AFC")
            iteration(NC - 1, 1, "FC")
            iteration(NC, 0, "C")

        @block.vector
        def _(dve):
            done = [0]

            def link(ins):
                done[0] += 1
                ins.then_inc(s["dve_setup"], 1)
                dve.wait_ge(s["dve_setup"], done[0])

            V = nc.vector
            V.memset(xc[:], 0.0).then_inc(s["xc_cleared"], 1)
            V.memset(ones[:], 1.0)
            V.memset(wT[:], 0.0)
            V.memset(st_b_wide[:], 1.0)
            V.memset(r[:], -1.0).then_inc(s["dve_cleared"], 1)
            dve.wait_ge(s["consts"], 16 * 4)
            dve.wait_ge(s["dve_cleared"], 1)

            def row_stats(n, src):
                for j in range(NJ):
                    V.bn_stats(stats[:, j, :], src[:, j, :]).then_inc(s["stats_done"], 1)
                aggregate(n)

            def bn_stats(n, j):
                if j == 0:
                    wait_for(dve, "xa_in", 16 * NJ, n, 0)
                V.bn_stats(stats[:, j, :], xa[:, j, :]).then_inc(s["stats_done"], 1)

            def aggregate(n):
                wait_for(dve, "stats_done", NJ, n, NJ)
                wait_for(dve, "ln_done", LN_OPS, n, 0)
                hold(dve)
                for j in range(NJ):
                    V.bn_aggr(mv[:, j, :], stats[:, j, :]).then_inc(s["mv_done"], 1)

            link(V.tensor_scalar(vec[:, vcol["conv_w1"], :], vec[:, vcol["conv_w1"], :], 1.0, None, ALU.add))
            assert done[0] == SETUP_VEC
            link(V.tensor_scalar(As[:].rearrange("p a b -> p (a b)"), small[:, 0:2 * S], sm("dt"), None, ALU.mult))
            link(V.tensor_reduce(absrow[:, 0:1], As[:, 0, :], AX_X, ALU.add, apply_absolute_value=True))
            dve.wait_ge(s["pe_setup"], 1)
            link(V.tensor_reduce(absrow[0:1, 1:2], banks[7][0:1, 0:S], AX_X, ALU.max))
            dve.wait_ge(s["pe_setup"], 2)
            link(V.tensor_copy(absrow[:, 2:3], banks[7][0:S, 0:1]))
            link(V.tensor_scalar(mask[:], sm("pow"), absrow[:, 2:3], None, ALU.is_lt))
            link(V.tensor_scalar(pick[:], mask[:], -1.0, 1.0, ALU.mult, ALU.add))
            link(V.tensor_tensor(pick[:], pick[:], sm("inv"), ALU.add))
            link(V.tensor_reduce(absrow[:, 3:4], pick[:], AX_X, ALU.min))
            link(V.tensor_scalar(absrow[:, 4:5], absrow[:, 3:4], 1.0, None, ALU.min))
            link(V.tensor_scalar(As[:].rearrange("p a b -> p (a b)"), As[:].rearrange("p a b -> p (a b)"),
                                 absrow[:, 4:5], None, ALU.mult))
            link(V.tensor_copy(XX[:, 0, :], ident[0:S, 0:S]))
            assert done[0] == SETUP_SERIES
            dve.wait_ge(s["halo_in"], 16 * 4 * B)
            row_stats(0, xc)
            for n in range(TERMS, 0, -1):
                dve.wait_ge(s["pe_setup"], 3 + TERMS - n)
                link(V.scalar_tensor_tensor(out=XX[:, 0, :], in0=banks[7][0:S, 0:S], scalar=1.0 / n,
                                            in1=ident[0:S, 0:S], op0=ALU.mult, op1=ALU.add))
            dve.wait_ge(s["xa_in"], 16 * NJ)
            row_stats(1, xa)
            dve.wait_ge(s["pe_setup"], 3 + TERMS)
            link(V.tensor_copy(XX[:, 1, :], banks[7][0:S, 0:S]))
            for n in range(SQUARINGS):
                if n == SQUARINGS - 7:
                    dve.wait_ge(s["y_done"], KH)
                    for k in range(KH):
                        V.memset(halo[:, k, :, 0, 0], 0.0)
                        ins = V.memset(halo[:, k, :, 1, NC - 1], 0.0)
                    ins.then_inc(s["halo_zeroed"], 1)
                dve.wait_ge(s["pe_setup"], 4 + TERMS + n)
                link(V.copy_predicated(XX[:].rearrange("p a b -> p (a b)"),
                                       mask[:, n:n + 1].bitcast(I32).to_broadcast([S, 2 * S]),
                                       banks[7][0:S, 0:2 * S]))
            link(V.tensor_reduce(absrow[:, 5:6], XX[:, 0, :], AX_X, ALU.add))
            link(V.tensor_scalar(absrow[:, 6:7], absrow[:, 5:6], -1.0 / S, None, ALU.mult))
            link(V.tensor_scalar(AC[:], XX[:, 0, :], absrow[:, 6:7], None, ALU.add))
            link(V.tensor_scalar(M[:], AC[:], sm("st_g"), None, ALU.mult))
            link(V.tensor_scalar(st_b_wide[:], st_b_wide[:], sm("st_b"), None, ALU.mult))
            link(V.tensor_reduce(absrow[0:1, 7:8], Bb[:], AX_X, ALU.add))
            link(V.tensor_scalar(absrow[0:1, 7:8], absrow[0:1, 7:8], -1.0 / S, None, ALU.mult))
            link(V.tensor_scalar(Bb[:], Bb[:], absrow[0:1, 7:8], None, ALU.add))
            dve.wait_ge(s["weights_in"], 16 * 7)
            link(V.tensor_reduce(btmp[:], BT[:], AX_X, ALU.add))
            link(V.tensor_scalar(btmp[:], btmp[:], -1.0 / S, None, ALU.mult))
            link(V.tensor_tensor(BT[:], BT[:], btmp[:].unsqueeze(2).to_broadcast([P, KH, S]), ALU.add))
            assert done[0] == SETUP_M
            dve.wait_ge(s["pe_setup"], SQ_END + 1)
            link(V.tensor_copy(dbias[:], banks[7][0:S, 0:1]))
            for k in range(KH):
                dve.wait_ge(s["wprime_mm"], k + 1)
                V.tensor_tensor(WT[:, k, :], WT[:, k, :], wbank[k][:], ALU.add).then_inc(s["wprime_done"], 1)

            def left_tap(c, k):
                wait_for(dve, "t1_done", KH, c, k + 1)
                if k == 0:
                    wait_for(dve, "halo_y", 1, c, 1)
                bank = cbank[k % 2][:].rearrange("p (b t) -> p b t", b=B)
                V.scalar_tensor_tensor(out=bank, in0=y[:, k, :, 0:CT], scalar=v_("conv_w0", k), in1=bank,
                                       op0=ALU.mult, op1=ALU.add).then_inc(s["conv_half"], 1)

            def right_tap(c, k, p):
                wait_for(dve, "conv_half", KH, c, k + 1)
                bank = cbank[k % 2][:].rearrange("p (b t) -> p b t", b=B)
                V.scalar_tensor_tensor(out=xnorm[p][:, k, :].rearrange("p (b t) -> p b t", b=B),
                                       in0=y[:, k, :, 2:CT + 2], scalar=v_("conv_w2", k), in1=bank,
                                       op0=ALU.mult, op1=ALU.add).then_inc(s["xnorm_done"], 1)

            def gated_x(c, m, p):
                wait_for(dve, "igs_done", KH, c, m + 1)
                if m == 0:
                    wait_for(dve, "b_mm", 1, c, 0)
                    wait_for(dve, "xnorm_done", KH, c, KH)
                V.tensor_tensor(xg[:, m, :], mbank["ig", m][:], xnorm[p][:, m, :],
                                ALU.mult).then_inc(s["xg_done"], 1)

            def silu(c, m, p):
                wait_for(dve, "sigf_done", KH, c, m + 1)
                V.scalar_tensor_tensor(out=G[p][:, m, :], in0=mbank["ffn", m][:], scalar=v_("ffn_b", m),
                                       in1=sigf[:, m % 2, :], op0=ALU.add, op1=ALU.mult
                                       ).then_inc(s["silu_done"], 1)

            def whole_gate(c, m, p):
                wait_for(dve, "gates_done", KH, c, m + 1)
                wait_for(dve, "silu_done", KH, c, m + 1)
                V.tensor_tensor(G[p][:, m, :], mbank["gate", m][:], G[p][:, m, :],
                                ALU.mult).then_inc(s["g_done"], 1)

            def state_times_c(c, p):
                wait_for(dve, "sn_done", 1, c, 1)
                wait_for(dve, "cT_done", 1, c, 1)
                wait_for(dve, "ssm_mm", KH, c, 0)
                V.tensor_tensor(ys[:], tbank["wr", 0][0:S, :], cT[p][:], ALU.mult).then_inc(s["ys_done"], 1)

            def gated_ssm(c, m, p):
                wait_for(dve, "ssm_mm", KH, c, m + 1)
                if m == 0:
                    wait_for(dve, "g_done", KH, c, KH)
                    wait_for(dve, "ofill", NJ, c, 0)
                V.scalar_tensor_tensor(out=sgT[:, m, :], in0=mbank["ssm", m][:], scalar=v_("D_b", m),
                                       in1=G[p][:, m, :], op0=ALU.add, op1=ALU.mult
                                       ).then_inc(s["sg_done"], 1)

            def add_x(c, j):
                wait_for(dve, "ofill", NJ, c, j + 1)
                wait_for(dve, OUT[j % 2], 8 * NJ, c, 16 * (j // 2))
                if j == 0:
                    wait_for(dve, "xc_in", 16 * NJ, c, 16 * NJ)
                V.tensor_tensor(o[:, j % 2, :], tbank["o", j][:], xc[:, j, :],
                                ALU.add).then_inc(s["o_done"], 1)

            def step(i, p, t):
                if t == 0:
                    wait_for(dve, "d_in", 16 * NJ, i, 16 * NJ)
                wait_for(dve, "p_ready", CT, i, t + 1)
                wait_for(dve, "r_ready", CT, i, t)
                w = dw[p][0:B, t, :]
                V.scalar_tensor_tensor(out=w, in0=scanP[0:B, 0:S], scalar=r[:], in1=w,
                                       op0=ALU.mult, op1=ALU.add).then_inc(s["w_ready"], 1)
                wait_for(dve, "w_ready", CT, i, t + 1)
                V.tensor_tensor_reduce(wq[:], w, w, 1.0 / S, EPS, ALU.mult, ALU.add,
                                       q[:]).then_inc(s["q_ready"], 1)
                V.transpose(wT[:], dw[p][:, t, :]).then_inc(s["wT_ready"], 1)

            for k in range(KH):
                left_tap(0, k)
                right_tap(0, k, 0)
            for j in range(NJ):
                bn_stats(2, j)
            aggregate(2)
            for m in range(KH):
                gated_x(0, m, 0)

            def iteration(i, p, parts):
                A, F, C = ("A" in parts), ("F" in parts), ("C" in parts)
                for t in range(CT):
                    if F:
                        step(i, p, t)
                    if "S" in parts:
                        if t in V_STATS:
                            bn_stats(i + 3, V_STATS.index(t))
                        if t == V_AGGR:
                            aggregate(i + 3)
                    if A:
                        if t in V_CONV:
                            k, second = divmod(V_CONV.index(t), 2)
                            if second:
                                right_tap(i + 1, k, 1 - p)
                            else:
                                left_tap(i + 1, k)
                        if t in V_XG:
                            gated_x(i + 1, V_XG.index(t), 1 - p)
                    if F:
                        if t in V_SILU:
                            silu(i, V_SILU.index(t), p)
                        if t in V_G:
                            whole_gate(i, V_G.index(t), p)
                    if C:
                        if t == V_YS:
                            state_times_c(i - 1, 1 - p)
                        if t in V_SG:
                            gated_ssm(i - 1, V_SG.index(t), 1 - p)
                        if t in V_ADD:
                            add_x(i - 1, V_ADD.index(t))

            iteration(0, 0, "ASF")
            iteration(1, 1, "ASFC")
            with dve.Fori(1, NC // 2 - 1) as pair:
                i = dve.snap(2 * pair)
                iteration(i, 0, "ASFC")
                iteration(i + 1, 1, "ASFC")
            iteration(NC - 2, 0, "AFC")
            iteration(NC - 1, 1, "FC")
            iteration(NC, 0, "C")

        @block.tensor
        def _(pe):
            mm = nc.tensor.matmul
            tp = nc.tensor.transpose

            def fill_z(c, k, i, middle):
                wait_for(pe, "z_done", NJ, c + 1, NJ)
                wait_bank(pe, T_USERS, "z", k, i, middle)
                for j in range(NJ):
                    ins = tp(tbank["z", k][:, P * j:P * j + P], z[:, j, P * k:P * k + P], ident[:])
                ins.then_inc(s["zfill"], 1)

            def fill_x(c, k, i, middle):
                wait_for(pe, "xn_done", NJ, c, NJ)
                wait_bank(pe, T_USERS, "x", k, i, middle)
                for j in range(NJ):
                    ins = tp(tbank["x", k][:, P * j:P * j + P], z[:, j, P * k:P * k + P], ident[:])
                ins.then_inc(s["xfill"], 1)

            def fill_w(c, j, i, middle):
                if j == 0:
                    wait_for(pe, "wr_done", NJ, c, NJ)
                    wait_bank(pe, T_USERS, "wr", 0, i, middle)
                    hold(pe)
                ins = tp(tbank["wr", 0][0:S, P * j:P * j + P], wr[:, j, :], ident[:])
                if j == NJ - 1:
                    ins.then_inc(s["wrfill"], 1)

            def fill_o(c, j, m, i, middle):
                if m == 0:
                    wait_for(pe, "sg_done", KH, c, KH)
                    wait_bank(pe, T_USERS, "o", j, i, middle)
                ins = tp(tbank["o", j][:, P * m:P * m + P], sgT[:, m, P * j:P * j + P], ident[:])
                if m == KH - 1:
                    ins.then_inc(s["ofill"], 1)

            def fill_d(c, j, i, middle):
                if j == 0:
                    wait_for(pe, "dT_done", 1, c, 1)
                    wait_bank(pe, T_USERS, "d", 0, i, middle)
                    hold(pe)
                ins = tp(tbank["d", 0][:, S * j:S * j + S], dT[:, P * j:P * j + P], ident[0:S, 0:S])
                if j == NJ - 1:
                    ins.then_inc(s["dfill"], 1)

            def ffn(c, m, k, i, middle):
                if k == 0:
                    wait_for(pe, "xnT_done", KH, c, KH)
                    wait_bank(pe, M_USERS, "ffn", m, i, middle)
                ins = mm(mbank["ffn", m][:], WT[:, k, P * m:P * m + P], xnT[:, k, :],
                         start=(k == 0), stop=(k == KH - 1))
                if k == KH - 1:
                    ins.then_inc(s["ffn_mm"], 1)

            def gate(c, m, k, p, i, middle):
                if k == 0:
                    wait_bank(pe, M_USERS, "gate", m, i, middle)
                ins = mm(mbank["gate", m][:], gateT[:, k, P * m:P * m + P], xnorm[p][:, k, :],
                         start=(k == 0), stop=(k == KH - 1))
                if k == KH - 1:
                    ins.then_inc(s["gate_mm"], 1)

            def in_gate(c, m, k, p, i, middle):
                if k == 0:
                    wait_for(pe, "xnorm_done", KH, c, KH)
                    wait_bank(pe, M_USERS, "ig", m, i, middle)
                ins = mm(mbank["ig", m][:], gateT[:, k, H + P * m:H + P * m + P], xnorm[p][:, k, :],
                         start=(k == 0), stop=(k == KH - 1))
                if k == KH - 1:
                    ins.then_inc(s["ig_mm"], 1)

            def b_proj(c, k, i, middle):
                if k == 0:
                    wait_bank(pe, M_USERS, "b", 0, i, middle)
                wait_for(pe, "xg_done", KH, c, k + 1)
                ins = mm(mbank["b", 0][0:S, :], BT[:, k, :], xg[:, k, :], start=(k == 0), stop=(k == KH - 1))
                if k == KH - 1:
                    ins.then_inc(s["b_mm"], 1)

            def c_proj(c, k, p, i, middle):
                if k == 0:
                    wait_bank(pe, M_USERS, "c", 0, i, middle)
                ins = mm(mbank["c", 0][0:S, :], CwT[:, k, :], xnorm[p][:, k, :],
                         start=(k == 0), stop=(k == KH - 1))
                if k == KH - 1:
                    ins.then_inc(s["c_mm"], 1)

            def ssm(c, m, i, middle):
                if m == 0:
                    wait_for(pe, "ys_done", 1, c, 1)
                wait_bank(pe, M_USERS, "ssm", m, i, middle)
                mm(mbank["ssm", m][:], DT[:, P * m:P * m + P], ys[:],
                   start=True, stop=True).then_inc(s["ssm_mm"], 1)

            def step(i, t):
                wait_for(pe, "wT_ready", CT, i, t + 1)
                hold(pe)
                mm(scanP[0:B, 0:S], wT[:, 0:B], M2[:, 0, :], start=True, stop=False)
                mm(scanP[0:B, 0:S], wT[:, 32:32 + B], M2[:, 1, :], start=False, stop=True
                   ).then_inc(s["p_ready"], 1)

            pe.wait_ge(s["consts"], 16 * 4)
            pe.wait_ge(s["dve_setup"], SETUP_VEC + 2)
            tp(banks[7][0:1, 0:S], absrow[:, 0:1], ident[0:S, 0:S]).then_inc(s["pe_setup"], 1)
            pe.wait_ge(s["dve_setup"], SETUP_VEC + 3)
            mm(banks[7][0:S, 0:1], ones[0:1, 0:S], absrow[0:1, 1:2], start=True, stop=True
               ).then_inc(s["pe_setup"], 1)
            for n in range(TERMS):
                pe.wait_ge(s["dve_setup"], SETUP_SERIES + n)
                mm(banks[7][0:S, 0:S], As[:, 1, :], XX[:, 0, :], start=True, stop=True
                   ).then_inc(s["pe_setup"], 1)
            pe.wait_ge(s["dve_setup"], SETUP_SERIES + TERMS)
            tp(banks[7][0:S, 0:S], XX[:, 0, :], ident[0:S, 0:S]).then_inc(s["pe_setup"], 1)
            for k in range(KH):
                fill_z(-1, k, -2, False)
            for n in range(SQUARINGS):
                if n == SQUARINGS - 6:
                    for k in range(KH):
                        fill_z(0, k, -1, False)
                pe.wait_ge(s["dve_setup"], SETUP_SERIES + TERMS + 1 + n)
                mm(banks[7][0:S, 0:S], XX[:, 1, :], XX[:, 0, :], start=True, stop=True)
                mm(banks[7][0:S, S:2 * S], XX[:, 0, :], XX[:, 1, :], start=True, stop=True
                   ).then_inc(s["pe_setup"], 1)
            pe.wait_ge(s["dve_setup"], SETUP_M)
            mm(banks[7][0:S, 0:1], AC[:], sm("st_b"), start=True, stop=False)
            mm(banks[7][0:S, 0:1], Bb[:], ones[0:1, 0:1], start=False, stop=True).then_inc(s["pe_setup"], 1)
            mm(scanP[0:B, 0:S], st_b_wide[:, 0:B], AC[:], start=True, stop=True).then_inc(s["p_ready"], 1)
            pe.wait_ge(s["dve_setup"], SETUP_M + 1)
            for k in range(KH):
                if k == KH - 1:
                    pe.wait_ge(s["wprime_done"], 1)
                mm(wbank[k][:], VT[:, P * k:P * k + P], CrT[:], start=True, stop=True
                   ).then_inc(s["wprime_mm"], 1)
            pe.wait_ge(s["m2_in"], 32)
            for k in range(KH):
                fill_x(0, k, -1, False)
            pe.wait_ge(s["wprime_done"], KH)
            for m in range(KH):
                for k in range(KH):
                    in_gate(0, m, k, 0, -1, False)
            for k in range(KH):
                b_proj(0, k, -1, False)
            for j in range(NJ):
                fill_d(0, j, -1, False)
            for k in range(KH):
                c_proj(0, k, 0, -1, False)

            def iteration(i, p, parts, middle):
                A, F, C = ("A" in parts), ("F" in parts), ("C" in parts)
                for t in range(CT):
                    if F:
                        step(i, t)
                        if t in PE_FFN:
                            ffn(i, *divmod(PE_FFN.index(t), KH), i, middle)
                    if C:
                        if t in PE_W:
                            fill_w(i - 1, PE_W.index(t), i, middle)
                        if t in PE_SSM:
                            ssm(i - 1, PE_SSM.index(t), i, middle)
                    if A:
                        for k in range(KH):
                            if PE_Z[k] == t:
                                fill_z(i + 1, k, i, middle)
                            if PE_X[k] == t:
                                fill_x(i + 1, k, i, middle)
                    if F and t in PE_GATE:
                        m, k = divmod(PE_GATE.index(t), KH)
                        gate(i, m, k, p, i, middle)
                    if C and t in PE_O:
                        fill_o(i - 1, *divmod(PE_O.index(t), KH), i, middle)
                    if A:
                        if t in PE_IG:
                            in_gate(i + 1, *divmod(PE_IG.index(t), KH), 1 - p, i, middle)
                        if t in PE_B:
                            b_proj(i + 1, PE_B.index(t), i, middle)
                        if t in PE_D:
                            fill_d(i + 1, PE_D.index(t), i, middle)
                        if t in PE_C:
                            c_proj(i + 1, PE_C.index(t), 1 - p, i, middle)

            iteration(0, 0, "ASF", False)
            iteration(1, 1, "ASFC", False)
            with pe.Fori(1, NC // 2 - 1) as pair:
                i = pe.snap(2 * pair)
                iteration(i, 0, "ASFC", True)
                iteration(i + 1, 1, "ASFC", True)
            iteration(NC - 2, 0, "AFC", False)
            iteration(NC - 1, 1, "FC", False)
            iteration(NC, 0, "C", False)


LN_OPS = 12
SETUP_VEC = 1
SETUP_SERIES = SETUP_VEC + 11
SETUP_M = SETUP_SERIES + TERMS + 1 + SQUARINGS + 11
SQ_END = 3 + TERMS + SQUARINGS


def kernel(**inputs):
    import concourse.bacc as _bacc
    from concourse.bass_utils import run_bass_kernel_spmd as _run

    a = {k: np.asarray(v) for k, v in inputs.items()}
    at = {k[len("L0_attn_"):]: v for k, v in a.items() if k.startswith("L0_attn_")}
    blocks = lambda v: v.reshape(KH, P).T
    conv = at["conv_w"].reshape(H, 3)
    parts = {"ln_g": at["ln_in_g"], "ln_b": at["ln_in_b"], "conv_w0": conv[:, 0], "conv_w1": conv[:, 1],
             "conv_w2": conv[:, 2], "conv_b": at["conv_b"], "gate_b": at["gate_b"][:H],
             "in_gate_b": at["gate_b"][H:], "ffn_b": a["L0_ffn_b"], "D_b": at["D_b"]}
    vec = np.stack([blocks(parts[n]) for n in VEC], axis=1)
    powers = np.float32(2.0) ** np.arange(SQUARINGS, dtype=np.float32)
    halves = np.float32(0.5) ** np.arange(1, SQUARINGS + 1, dtype=np.float32)
    small = np.concatenate([
        at["A"], at["A"].T, at["ln_st_g"][:, None], at["ln_st_b"][:, None], at["C_b"][:, None],
        np.broadcast_to(at["dt_A"].reshape(1, 1), (S, 1)),
        np.broadcast_to(powers, (S, SQUARINGS)), np.broadcast_to(halves, (S, SQUARINGS))], axis=1)
    arrays = {
        "x": at["x"], "ident": np.eye(P, dtype=np.float32), "gateT": at["gate_w"].T, "WT": a["L0_ffn_W"].T,
        "VT": a["L0_ffn_V_r"].T, "CrT": a["L0_ffn_C"].T, "BT": at["B_w"].T, "CwT": at["C_w"].T,
        "DT": at["D_w"].T, "vec": vec, "small": small, "Bb": at["B_b"].reshape(1, S),
    }
    nc = _bacc.Bacc("TRN2", target_bir_lowering=False, num_devices=1)
    held, args = {}, []
    for name, v in arrays.items():
        v = np.ascontiguousarray(v)
        held[f"in_{name}"] = v
        args.append(nc.dram_tensor(f"in_{name}", v.shape, mybir.dt.from_np(v.dtype), kind="ExternalInput").ap())
    out = nc.dram_tensor("out_0", (B, T, H), F32, kind="ExternalOutput").ap()
    build(nc, *args, out)
    r = _run(nc, [held], core_ids=[0])
    return r.results[0]["out_0"]
```

```python
from contextlib import ExitStack

import numpy as np

import concourse.bass as bass
from concourse import mybir

ALU = mybir.AluOpType
ACT = mybir.ActivationFunctionType
F32 = mybir.dt.float32
I32 = mybir.dt.int32
AX_X = mybir.AxisListType.X

P = 128
B = 8
T = 2048
H = 512
S = 64
R = 32
KH = H // P
CT = 64
NC = T // CT
TOK = B * CT
NJ = TOK // P
BJ = B // NJ
EPS = 1e-5
SQUARINGS = 20
TERMS = 12

OUT = ["out_even", "out_odd"]

VEC = ["ln_g", "ln_b", "conv_w0", "conv_w1", "conv_w2", "conv_b", "gate_b", "in_gate_b", "ffn_b", "D_b"]
SMALL = {"A": (0, S), "AT": (S, S), "st_g": (2 * S, 1), "st_b": (2 * S + 1, 1), "C_b": (2 * S + 2, 1),
         "dt": (2 * S + 3, 1), "pow": (2 * S + 4, SQUARINGS), "inv": (2 * S + 4 + SQUARINGS, SQUARINGS)}
SMALL_W = 2 * S + 4 + 2 * SQUARINGS

T_USERS = [("z", k, "A") for k in range(KH)] + [("wr", 0, "C")] + [("x", k, "A") for k in range(KH)] \
    + [("o", j, "C") for j in range(NJ)] + [("d", 0, "A")]
M_USERS = [("ffn", m, "F") for m in range(KH)] + [("ssm", m, "C") for m in range(KH)] \
    + [("ig", m, "A") for m in range(KH)] + [("b", 0, "A")] + [("gate", m, "F") for m in range(KH)] \
    + [("c", 0, "A")]

PE_Z = (3, 3, 6, 6)
PE_FFN = (0, 1, 2, 4) + (5, 7, 8, 9) + tuple(range(10, 18))
PE_W = range(11, 15)
PE_X = (18, 18, 21, 21)
PE_SSM = (19, 20, 22, 23)
PE_IG = range(24, 40)
PE_O = range(27, 43)
PE_B = range(40, 44)
PE_GATE = range(44, 60)
PE_D = range(46, 50)
PE_C = range(60, 64)
V_CONV = (7, 8, 9, 10, 12, 13, 14, 15)
V_SILU = (11, 16, 18, 20)
V_YS = 17
V_SG = (21, 22, 24, 25)
V_STATS = (26, 27, 28, 30)
V_AGGR = 31
V_XG = (29, 33, 37, 41)
V_ADD = (32, 36, 40, 44)
V_G = (49, 53, 57, 61)
POOL_RS = (7, 8, 9)
POOL_LN = (36, 36, 37, 38, 39, 40, 41, 42, 43, 44, 44, 45)
PE_IG_FIRST = (19, 20, 22, 23) + (25, 26, 27, 28) + (30, 31, 32, 33) + (35, 36, 37, 38)
PE_GATE_LAST = (27, 28, 29, 31) + (32, 34, 35, 37) + (38, 40, 41, 43) + (44, 46, 47, 49)
V_G_LAST = (33, 39, 45, 51)

PE_WPRIME = (0, 1, 4, 5)
DVE_WPRIME = (1, 2, 5, 6)
PE_HALO = (2, 2, 3, 3)
DVE_EDGES = 6
PE_Z0 = (6, 6, 7, 7)
DVE_CONV = (8, 9, 10, 11)
PE_IG0 = (12, 13, 14, 15, 16, 16, 17, 17, 18, 18, 19, 19)
PE_X0 = (16, 16, 18, 18)
DVE_XG0 = (17, 19)
DVE_STATS2 = (14, 15, 16, 18)


def build(nc, x, ident_d, gateT_d, WT_d, VT_d, CrT_d, BT_d, CwT_d, DT_d, vec_d, small_d, Bb_d, out):
    with ExitStack() as ctx:
        def sb(name, shape, dt=F32):
            return ctx.enter_context(nc.sbuf_tensor(name, shape, dt))

        def sem(name):
            return ctx.enter_context(nc.semaphore(name))

        ident = sb("ident", [P, P])
        gateT = sb("gateT", [P, KH, 2 * H])
        WT = sb("WT", [P, KH, H])
        VT = sb("VT", [R, H])
        CrT = sb("CrT", [R, H])
        BT = sb("BT", [P, KH, S])
        CwT = sb("CwT", [P, KH, S])
        DT = sb("DT", [S, H])
        vec = sb("vec", [P, len(VEC), KH])
        small = sb("small", [S, SMALL_W])
        Bb = sb("Bb", [1, S])
        ones = sb("ones", [1, P])
        minus_half = sb("minus_half", [P, NJ])
        dbias = sb("dbias", [S, 1])
        btmp = sb("btmp", [P, KH])
        As = sb("As", [S, 2, S])
        absrow = sb("absrow", [S, 8])
        XX = sb("XX", [S, 2, S])
        mask = sb("mask", [S, SQUARINGS])
        pick = sb("pick", [S, SQUARINGS])
        AC = sb("AC", [S, S])
        M = sb("M", [S, S])
        M2 = sb("M2", [32, 2, S])
        st_b_wide = sb("st_b_wide", [S, P])
        xa = sb("xa", [P, NJ, H])
        xc = sb("xc", [P, NJ, H])
        stats = sb("stats", [P, NJ, 6])
        mv = sb("mv", [P, NJ, 2])
        ln = sb("ln", [P, 8, NJ])
        z = sb("z", [P, NJ, H])
        y = sb("y", [P, KH, B, CT + 2])
        halo = sb("halo", [P, KH, B, 2 * NC + 2])
        xnT = sb("xnT", [P, KH, TOK])
        xnorm = [sb(f"xnorm{p}", [P, KH, TOK]) for p in range(2)]
        xg = sb("xg", [P, KH, TOK])
        sigf = sb("sigf", [P, 2, TOK])
        G = [sb(f"G{p}", [P, KH, TOK]) for p in range(2)]
        cT = [sb(f"cT{p}", [S, TOK]) for p in range(2)]
        dT = sb("dT", [S, TOK])
        dtok = sb("dtok", [P, NJ, S])
        dw = [sb(f"dw{p}", [32, CT, S + 1]) for p in range(2)]
        wtok = sb("wtok", [P, NJ, S])
        wsq = sb("wsq", [P, NJ, S])
        ssq = sb("ssq", [P, 3, NJ])
        wr = sb("wr", [P, NJ, S])
        ys = sb("ys", [S, TOK])
        sgT = sb("sgT", [P, KH, TOK])
        o = sb("o", [P, 2, H])
        wT = sb("wT", [32, S])
        wq = sb("wq", [B, S + 1])
        q = sb("q", [B, 1])
        r = sb("r", [B, 1])

        banks = [ctx.enter_context(nc.psum_tensor(f"bank{n}", [P, TOK], F32)) for n in range(8)]
        scanP = banks[0]
        tbank = {}
        for n, (what, k, _) in enumerate(T_USERS):
            tbank[what, k] = banks[1 + n % 2]
        mbank = {}
        for n, (what, k, _) in enumerate(M_USERS):
            mbank[what, k] = banks[[3, 4, 7][n % 3]]
        cbank = [banks[5], banks[6]]
        wbank = [banks[5 + k % 2] for k in range(KH)]

        names = """held consts bt_in gate_in weights_in halo_in xa_in xc_in d_in w_in out_even out_odd dve_cleared pool_cleared pe_setup dve_setup halo_zeroed xc_cleared m2_in wprime_mm wprime_done bt_steps
            p_ready r_ready w_ready q_ready wT_ready
            stats_done mv_done ln_done z_done zfill y_done halo_y t1_done conv_half xnorm_done xn_done xfill xnT_done
            ig_mm igs_done xg_done b_mm dT_done dfill dtok_done c_mm cT_done
            ffn_mm ffn_biased ssm_biased silu_done gate_mm gates_done g_done
            ssq_done rs_done wr_done wrfill sn_done ys_done ssm_mm sg_done ofill o_done""".split()
        s = {n: sem(n) for n in names}

        vcol = {n: i for i, n in enumerate(VEC)}

        def v_(name, k):
            return vec[:, vcol[name], k:k + 1]

        def sm(name):
            a, w = SMALL[name]
            return small[:, a:a + w]

        def released(user, i):
            what, k = user
            return {
                "z": lambda: ("y_done", KH, i + 2, k + 1),
                "x": lambda: ("xnT_done", KH, i + 1, k + 1),
                "wr": lambda: ("ys_done", 1, i, 0),
                "o": lambda: ("o_done", NJ, i - 1, k + 1),
                "ffn": lambda: ("silu_done", KH, i, k + 1),
                "gate": lambda: ("g_done", KH, i, k + 1),
                "ssm": lambda: ("sg_done", KH, i - 1, k + 1),
                "ig": lambda: ("xg_done", KH, i + 1, k + 1),
                "b": lambda: ("dT_done", 1, i + 1, 1),
                "d": lambda: ("dtok_done", 1, i + 1, 1),
                "c": lambda: ("cT_done", 1, i + 1, 1),
            }[what]()

        def parts_of(i, middle):
            if middle:
                return "AFC"
            return {-2: "z", -1: "A", 0: "AF", NC - 1: "FC", NC: "C"}.get(i, "AFC" if 0 < i < NC else "")

        def wait_for(eng, name, per, n, k):
            v = n * per + k
            if isinstance(v, int) and v <= 0:
                return
            eng.wait_ge(s[name], v)

        def hold(eng):
            eng.sem_inc(s["held"], 1)

        def wait_bank(eng, users, what, k, i, middle):
            n = [u[:2] for u in users].index((what, k))
            size = 2 if users is T_USERS else 3
            back, at = 0, n
            while back < 4:
                at -= 1
                if at < 0:
                    at, back = len(users) - 1, back + 1
                same = at % size == n % size
                parts = parts_of(i if middle else i - back, middle)
                here = users[at][2] in parts or (parts == "z" and users[at][0] == "z")
                if same and here:
                    wait_for(eng, *released(users[at][:2], i - back))
                    return

        block = ctx.enter_context(nc.Block())

        @block.sync
        def _(sp):
            def load_x(dst, c, name):
                for j in range(NJ):
                    sp.dma_start(dst[:, j, :],
                                 x[BJ * j:BJ * (j + 1), bass.ds(c * CT, CT), :]).then_inc(s[name], 16)

            for dst, src in [(small[:], small_d), (ident[:], ident_d), (vec[:], vec_d), (Bb[:], Bb_d)]:
                sp.dma_start(dst, src).then_inc(s["consts"], 16)
            sp.wait_ge(s["xc_cleared"], 1)
            for b in range(B):
                p0 = CT * (b % BJ)
                pairs = x[b, CT // 2:T - CT // 2, :].rearrange("(m r) h -> m r h", r=CT)
                sp.dma_start(xc[p0 + 2:p0 + CT, b // BJ, :],
                             pairs[:, CT // 2 - 1:CT // 2 + 1, :]).then_inc(s["halo_in"], 16)
            load_x(xa, 0, "xa_in")
            by_rows = lambda a: a.rearrange("(k p) n -> p k n", p=P)
            sp.dma_start(BT[:], by_rows(BT_d)).then_inc(s["bt_in"], 16)
            for dst, src in [(VT[:], VT_d), (CrT[:], CrT_d), (WT[:], by_rows(WT_d))]:
                sp.dma_start(dst, src).then_inc(s["weights_in"], 16)
            sp.dma_start(gateT[:], by_rows(gateT_d)).then_inc(s["gate_in"], 16)
            for dst, src in [(CwT[:], by_rows(CwT_d)), (DT[:], DT_d)]:
                sp.dma_start(dst, src).then_inc(s["gate_in"], 16)

            def send_d(c, p):
                if isinstance(c, int) and c == 0:
                    sp.wait_ge(s["pool_cleared"], 5)
                wait_for(sp, "dtok_done", 1, c, 1)
                hold(sp)
                wait_for(sp, "w_in", 16 * NJ, c - 1, 0)
                for j in range(NJ):
                    sp.dma_start(dw[p][BJ * j:BJ * (j + 1), :, 0:S], dtok[:, j, :]).then_inc(s["d_in"], 16)

            def send_w(c, p):
                wait_for(sp, "w_ready", CT, c, CT)
                hold(sp)
                wait_for(sp, "wr_done", NJ, c, 0)
                for j in range(NJ):
                    sp.dma_start(wtok[:, j, :], dw[p][BJ * j:BJ * (j + 1), :, 0:S]).then_inc(s["w_in"], 16)

            def prefetch_xa(c):
                wait_for(sp, "xn_done", NJ, c, 0)
                hold(sp)
                load_x(xa, c, "xa_in")

            def send_out(c, j):
                wait_for(sp, "o_done", NJ, c, j + 1)
                hold(sp)
                sp.dma_start(out[BJ * j:BJ * (j + 1), bass.ds(c * CT, CT), :],
                             o[:, j % 2, :]).then_inc(s[OUT[j % 2]], 16)

            prefetch_xa(1)
            sp.wait_ge(s["dve_setup"], SETUP_M - 4)
            for h in range(2):
                sp.dma_start(M2[:, h, :], M[32 * h:32 * h + 32, :]).then_inc(s["m2_in"], 16)
            send_d(0, 0)

            def iteration(i, p, parts, middle):
                if "C" in parts:
                    send_w(i - 1, 1 - p)
                if "A" in parts and (middle or i + 2 < NC):
                    prefetch_xa(i + 2)
                if "C" in parts:
                    for j in range(NJ):
                        send_out(i - 1, j)
                if "F" in parts:
                    wait_for(sp, "z_done", NJ, i, NJ)
                    hold(sp)
                    wait_for(sp, "o_done", NJ, i, 0)
                    hold(sp)
                    load_x(xc, i, "xc_in")
                if "A" in parts:
                    send_d(i + 1, 1 - p)

            iteration(0, 0, "ASF", False)
            iteration(1, 1, "ASFC", False)
            with sp.Fori(1, NC // 2 - 1) as pair:
                i = sp.snap(2 * pair)
                iteration(i, 0, "ASFC", True)
                iteration(i + 1, 1, "ASFC", True)
            iteration(NC - 2, 0, "AFC", False)
            iteration(NC - 1, 1, "FC", False)
            iteration(NC, 0, "C", False)
            for name in OUT:
                sp.wait_ge(s[name], 8 * NJ * NC)

        @block.gpsimd
        def _(pool):
            nc.gpsimd.memset(minus_half[:], -0.5).then_inc(s["pool_cleared"], 1)
            nc.gpsimd.memset(dw[0][:], 0.0).then_inc(s["pool_cleared"], 1)
            nc.gpsimd.memset(dw[1][:], 0.0).then_inc(s["pool_cleared"], 1)
            for p in range(2):
                pool.wait_ge(s["pool_cleared"], 2 + p)
                nc.gpsimd.memset(dw[p][0:B, :, S:S + 1], (S * EPS) ** 0.5).then_inc(s["pool_cleared"], 1)
            pool.wait_ge(s["dve_cleared"], 1)

            def step(i, t):
                wait_for(pool, "q_ready", CT, i, t + 1)
                nc.gpsimd.tensor_tensor(r[:], q[:], minus_half[0:B, 0:1], ALU.pow).then_inc(s["r_ready"], 1)

            def ln_op(n, k):
                mean, var = mv[:, :, 0], mv[:, :, 1]
                nm, a, r1, v2, r2, rr, bx, bz = (ln[:, a, :] for a in range(8))
                if k == 0:
                    wait_for(pool, "mv_done", NJ, n, NJ)
                    wait_for(pool, "xn_done", NJ, n - 1, 0)
                else:
                    wait_for(pool, "ln_done", LN_OPS, n, k)
                if k == 9:
                    wait_for(pool, "z_done", NJ, n, 0)
                hold(pool)
                g = nc.gpsimd
                ins = [
                    lambda: g.tensor_scalar(nm, mean, -1.0, None, ALU.mult),
                    lambda: g.tensor_scalar(a, var, EPS, None, ALU.add),
                    lambda: g.tensor_tensor(r1[:, 0:2], a[:, 0:2], minus_half[:, 0:2], ALU.pow),
                    lambda: g.tensor_tensor(r1[:, 2:4], a[:, 2:4], minus_half[:, 2:4], ALU.pow),
                    lambda: g.tensor_tensor(v2, var, r1, ALU.mult),
                    lambda: g.tensor_tensor(v2, v2, r1, ALU.mult),
                    lambda: g.tensor_scalar(a, v2, EPS, None, ALU.add),
                    lambda: g.tensor_tensor(r2[:, 0:2], a[:, 0:2], minus_half[:, 0:2], ALU.pow),
                    lambda: g.tensor_tensor(r2[:, 2:4], a[:, 2:4], minus_half[:, 2:4], ALU.pow),
                    lambda: g.tensor_tensor(rr, r1, r2, ALU.mult),
                    lambda: g.tensor_tensor(bx, nm, r1, ALU.mult),
                    lambda: g.tensor_tensor(bz, nm, rr, ALU.mult),
                ][k]()
                ins.then_inc(s["ln_done"], 1)

            def state_scale(c, k):
                if k == 0:
                    wait_for(pool, "ssq_done", NJ, c, NJ)
                    hold(pool)
                    nc.gpsimd.tensor_scalar(ssq[:, 1, :], ssq[:, 0, :], EPS, None,
                                            ALU.add).then_inc(s["rs_done"], 1)
                else:
                    wait_for(pool, "rs_done", 3, c, k)
                    wait_for(pool, "wr_done", NJ, c, 0)
                    half = slice(2 * k - 2, 2 * k)
                    nc.gpsimd.tensor_tensor(ssq[:, 2, half], ssq[:, 1, half], minus_half[:, half],
                                            ALU.pow).then_inc(s["rs_done"], 1)

            for n in range(3):
                for k in range(LN_OPS):
                    ln_op(n, k)

            def iteration(i, parts):
                for t in range(CT):
                    if "F" in parts:
                        step(i, t)
                    if "C" in parts and t in POOL_RS:
                        state_scale(i - 1, POOL_RS.index(t))
                    if "S" in parts:
                        for k in range(LN_OPS):
                            if POOL_LN[k] == t:
                                ln_op(i + 3, k)

            iteration(0, "ASF")
            iteration(1, "ASFC")
            with pool.Fori(1, NC // 2 - 1) as pair:
                i = pool.snap(2 * pair)
                iteration(i, "ASFC")
                iteration(i + 1, "ASFC")
            iteration(NC - 2, "AFC")
            iteration(NC - 1, "FC")
            iteration(NC, "C")

        @block.scalar
        def _(act):
            a_ = nc.scalar.activation

            def normalise_z(n, src=xa):
                wait_for(act, "ln_done", LN_OPS, n, LN_OPS)
                wait_for(act, "xfill", KH, n - 1, 0)
                for j in range(NJ):
                    a_(z[:, j, :], src[:, j, :], ACT.Identity, bias=ln[:, 7, j:j + 1],
                       scale=ln[:, 5, j:j + 1]).then_inc(s["z_done"], 1)

            def normalise_x(c, tiles):
                if tiles[0] == 0:
                    wait_for(act, "zfill", KH, c + 1, KH)
                for j in tiles:
                    a_(z[:, j, :], xa[:, j, :], ACT.Identity, bias=ln[:, 6, j:j + 1],
                       scale=ln[:, 2, j:j + 1]).then_inc(s["xn_done"], 1)

            def make_y(c, k):
                wait_for(act, "zfill", KH, c + 1, k + 1)
                wait_for(act, "xnorm_done", KH, c - 1, k + 1)
                a_(y[:, k, :, 1:CT + 1], tbank["z", k][:].rearrange("p (b t) -> p b t", b=B),
                   ACT.Identity, bias=v_("ln_b", k), scale=v_("ln_g", k)).then_inc(s["y_done"], 1)

            def copy_halo(c):
                wait_for(act, "xnorm_done", KH, c, 0)
                nc.scalar.copy(y[:, :, :, 0:CT + 2:CT + 1],
                               halo[:, :, :, bass.ds(2 * c, 2, 3)]
                               ).then_inc(s["halo_y"], 1)

            def centre_tap(c, k):
                wait_for(act, "y_done", KH, c + 1, k + 1)
                wait_for(act, "xnorm_done", KH, c, k - 1)
                a_(cbank[k % 2][:].rearrange("p (b t) -> p b t", b=B), y[:, k, :, 1:CT + 1],
                   ACT.Identity, bias=v_("conv_b", k), scale=v_("conv_w1", k)).then_inc(s["t1_done"], 1)

            def copy_xnT(c, k):
                wait_for(act, "xfill", KH, c, k + 1)
                wait_for(act, "ffn_mm", KH, c, 0)
                nc.scalar.copy(xnT[:, k, :], tbank["x", k][:]).then_inc(s["xnT_done"], 1)

            def input_gate(c, m):
                wait_for(act, "ig_mm", KH, c, m + 1)
                a_(mbank["ig", m][:], mbank["ig", m][:], ACT.Sigmoid,
                   bias=v_("in_gate_b", m)).then_inc(s["igs_done"], 1)

            def copy_c(c, p):
                wait_for(act, "c_mm", 1, c, 1)
                wait_for(act, "ys_done", 1, c - 1, 0)
                a_(cT[p][:], mbank["c", 0][0:S, :], ACT.Identity, bias=sm("C_b")).then_inc(s["cT_done"], 1)

            def copy_dT(c):
                wait_for(act, "b_mm", 1, c, 1)
                a_(dT[:], mbank["b", 0][0:S, :], ACT.Identity, bias=dbias[:]).then_inc(s["dT_done"], 1)

            def copy_dtok(c):
                wait_for(act, "dfill", 1, c, 1)
                wait_for(act, "d_in", 16 * NJ, c, 0)
                nc.scalar.copy(dtok[:].rearrange("p j e -> p (j e)"),
                               tbank["d", 0][:, 0:NJ * S]).then_inc(s["dtok_done"], 1)

            def ffn_sigmoid(c, m):
                wait_for(act, "ffn_mm", KH, c, m + 1)
                wait_for(act, "silu_done", KH, c, m - 1)
                a_(sigf[:, m % 2, :], mbank["ffn", m][:], ACT.Sigmoid,
                   bias=v_("ffn_b", m))
                a_(mbank["ffn", m][:], mbank["ffn", m][:], ACT.Identity,
                   bias=v_("ffn_b", m)).then_inc(s["ffn_biased"], 1)

            def ssm_bias(c, m):
                wait_for(act, "ssm_mm", KH, c, m + 1)
                a_(mbank["ssm", m][:], mbank["ssm", m][:], ACT.Identity,
                   bias=v_("D_b", m)).then_inc(s["ssm_biased"], 1)

            def gate_sigmoid(c, m):
                wait_for(act, "gate_mm", KH, c, m + 1)
                a_(mbank["gate", m][:], mbank["gate", m][:], ACT.Sigmoid,
                   bias=v_("gate_b", m)).then_inc(s["gates_done"], 1)

            def state_squares(c):
                wait_for(act, "w_in", 16 * NJ, c, 16 * NJ)
                wait_for(act, "rs_done", 3, c, 0)
                for j in range(NJ):
                    a_(wsq[:, j, :], wtok[:, j, :], ACT.Square, scale=float(S) ** -0.5,
                       accum_out=ssq[:, 0, j:j + 1]).then_inc(s["ssq_done"], 1)

            def state_normalise(c):
                wait_for(act, "rs_done", 3, c, 3)
                wait_for(act, "wrfill", 1, c, 0)
                for j in range(NJ):
                    a_(wr[:, j, :], wtok[:, j, :], ACT.Copy,
                       scale=ssq[:, 2, j:j + 1]).then_inc(s["wr_done"], 1)

            def state_affine(c):
                wait_for(act, "wrfill", 1, c, 1)
                bank = tbank["wr", 0][0:S, :]
                a_(bank, bank, ACT.Identity, bias=sm("st_b"), scale=sm("st_g")).then_inc(s["sn_done"], 1)

            act.wait_ge(s["dve_cleared"], 1)
            a_(sigf[0:1, 0, 0:1], ones[0:1, 0:1], ACT.Sigmoid)
            act.wait_ge(s["consts"], 16 * 4)
            act.wait_ge(s["dve_setup"], SETUP_VEC)
            normalise_z(0, xc)
            for k in range(KH):
                act.wait_ge(s["zfill"], k + 1)
                a_(halo[:, k, :, 0:2 * NC], tbank["z", k][:].rearrange("p (b m) -> p b m", b=B), ACT.Identity,
                   bias=v_("ln_b", k), scale=v_("ln_g", k)).then_inc(s["y_done"], 1)
            normalise_z(1)

            def first_taps(c):
                for k in range(2):
                    make_y(c, k)
                for k in range(2):
                    centre_tap(c, k)

            act.wait_ge(s["halo_zeroed"], 1)
            copy_halo(0)
            act.wait_ge(s["wprime_done"], KH)
            first_taps(0)
            for k in range(2, 4):
                make_y(0, k)
            for k in range(2, 4):
                centre_tap(0, k)
            normalise_x(0, range(NJ))
            for m in range(KH):
                if m < 2:
                    for k in range(2 * m, 2 * m + 2):
                        copy_xnT(0, k)
                input_gate(0, m)
            act.wait_ge(s["dve_setup"], SETUP_M + 1)
            copy_dT(0)
            copy_dtok(0)
            copy_c(0, 0)

            def iteration(i, p, parts):
                A, F, C = ("A" in parts), ("F" in parts), ("C" in parts)
                if A:
                    normalise_z(i + 2)
                    copy_halo(i + 1)
                    first_taps(i + 1)
                if C:
                    state_squares(i - 1)
                if F:
                    ffn_sigmoid(i, 0)
                if A:
                    for k in range(2, 4):
                        make_y(i + 1, k)
                    normalise_x(i + 1, (0, 1))
                    centre_tap(i + 1, 2)
                if C:
                    state_normalise(i - 1)
                if A:
                    normalise_x(i + 1, (2, 3))
                    centre_tap(i + 1, 3)
                if F:
                    ffn_sigmoid(i, 1)
                    ffn_sigmoid(i, 2)
                if C:
                    state_affine(i - 1)
                if F:
                    ffn_sigmoid(i, 3)
                for k in range(KH):
                    if A:
                        copy_xnT(i + 1, k)
                    if C and k == 1:
                        ssm_bias(i - 1, 0)
                        ssm_bias(i - 1, 1)
                for m in range(2, KH):
                    if C:
                        ssm_bias(i - 1, m)
                if A:
                    for m in range(KH):
                        input_gate(i + 1, m)
                    copy_dT(i + 1)
                if F:
                    gate_sigmoid(i, 0)
                if A:
                    copy_dtok(i + 1)
                if F:
                    for m in range(1, KH):
                        gate_sigmoid(i, m)
                if A:
                    copy_c(i + 1, 1 - p)

            iteration(0, 0, "ASF")
            iteration(1, 1, "ASFC")
            with act.Fori(1, NC // 2 - 1) as pair:
                i = act.snap(2 * pair)
                iteration(i, 0, "ASFC")
                iteration(i + 1, 1, "ASFC")
            iteration(NC - 2, 0, "AFC")
            iteration(NC - 1, 1, "FC")
            iteration(NC, 0, "C")

        @block.vector
        def _(dve):
            done = [0]

            def link(ins):
                done[0] += 1
                ins.then_inc(s["dve_setup"], 1)
                dve.wait_ge(s["dve_setup"], done[0])

            V = nc.vector
            V.memset(xc[:], 0.0).then_inc(s["xc_cleared"], 1)
            V.memset(ones[:], 1.0)
            V.memset(wT[:], 0.0)
            V.memset(st_b_wide[:], 1.0)
            V.memset(r[:], -1.0).then_inc(s["dve_cleared"], 1)
            dve.wait_ge(s["consts"], 16 * 4)
            dve.wait_ge(s["dve_cleared"], 1)

            def row_stats(n, src):
                for j in range(NJ):
                    V.bn_stats(stats[:, j, :], src[:, j, :]).then_inc(s["stats_done"], 1)
                aggregate(n)

            def bn_stats(n, j):
                if j == 0:
                    wait_for(dve, "xa_in", 16 * NJ, n, 0)
                V.bn_stats(stats[:, j, :], xa[:, j, :]).then_inc(s["stats_done"], 1)

            def aggregate(n):
                wait_for(dve, "stats_done", NJ, n, NJ)
                wait_for(dve, "ln_done", LN_OPS, n, 0)
                hold(dve)
                for j in range(NJ):
                    V.bn_aggr(mv[:, j, :], stats[:, j, :]).then_inc(s["mv_done"], 1)

            def left_tap(c, k):
                wait_for(dve, "t1_done", KH, c, k + 1)
                if k == 0:
                    wait_for(dve, "halo_y", 1, c, 1)
                bank = cbank[k % 2][:].rearrange("p (b t) -> p b t", b=B)
                V.scalar_tensor_tensor(out=bank, in0=y[:, k, :, 0:CT], scalar=v_("conv_w0", k), in1=bank,
                                       op0=ALU.mult, op1=ALU.add).then_inc(s["conv_half"], 1)

            def right_tap(c, k, p):
                wait_for(dve, "conv_half", KH, c, k + 1)
                bank = cbank[k % 2][:].rearrange("p (b t) -> p b t", b=B)
                V.scalar_tensor_tensor(out=xnorm[p][:, k, :].rearrange("p (b t) -> p b t", b=B),
                                       in0=y[:, k, :, 2:CT + 2], scalar=v_("conv_w2", k), in1=bank,
                                       op0=ALU.mult, op1=ALU.add).then_inc(s["xnorm_done"], 1)

            def gated_x(c, m, p):
                wait_for(dve, "igs_done", KH, c, m + 1)
                if m == 0:
                    wait_for(dve, "b_mm", 1, c, 0)
                    wait_for(dve, "xnorm_done", KH, c, KH)
                V.tensor_tensor(xg[:, m, :], mbank["ig", m][:], xnorm[p][:, m, :],
                                ALU.mult).then_inc(s["xg_done"], 1)

            def silu(c, m, p):
                wait_for(dve, "ffn_biased", KH, c, m + 1)
                V.tensor_tensor(G[p][:, m, :], mbank["ffn", m][:], sigf[:, m % 2, :],
                                ALU.mult).then_inc(s["silu_done"], 1)

            def whole_gate(c, m, p):
                wait_for(dve, "gates_done", KH, c, m + 1)
                wait_for(dve, "silu_done", KH, c, m + 1)
                V.tensor_tensor(G[p][:, m, :], mbank["gate", m][:], G[p][:, m, :],
                                ALU.mult).then_inc(s["g_done"], 1)

            def state_times_c(c, p):
                wait_for(dve, "sn_done", 1, c, 1)
                wait_for(dve, "cT_done", 1, c, 1)
                wait_for(dve, "ssm_mm", KH, c, 0)
                V.tensor_tensor(ys[:], tbank["wr", 0][0:S, :], cT[p][:], ALU.mult).then_inc(s["ys_done"], 1)

            def gated_ssm(c, m, p):
                wait_for(dve, "ssm_biased", KH, c, m + 1)
                if m == 0:
                    wait_for(dve, "g_done", KH, c, KH)
                    wait_for(dve, "ofill", NJ, c, 0)
                V.tensor_tensor(sgT[:, m, :], mbank["ssm", m][:], G[p][:, m, :],
                                ALU.mult).then_inc(s["sg_done"], 1)

            def add_x(c, j):
                wait_for(dve, "ofill", NJ, c, j + 1)
                wait_for(dve, OUT[j % 2], 8 * NJ, c, 16 * (j // 2))
                if j == 0:
                    wait_for(dve, "xc_in", 16 * NJ, c, 16 * NJ)
                V.tensor_tensor(o[:, j % 2, :], tbank["o", j][:], xc[:, j, :],
                                ALU.add).then_inc(s["o_done"], 1)

            def step(i, p, t):
                if t == 0:
                    wait_for(dve, "d_in", 16 * NJ, i, 16 * NJ)
                wait_for(dve, "p_ready", CT, i, t + 1)
                wait_for(dve, "r_ready", CT, i, t)
                w = dw[p][0:B, t, 0:S]
                w_eps = dw[p][0:B, t, :]
                V.scalar_tensor_tensor(out=w, in0=scanP[0:B, 0:S], scalar=r[:], in1=w,
                                       op0=ALU.mult, op1=ALU.add).then_inc(s["w_ready"], 1)
                wait_for(dve, "w_ready", CT, i, t + 1)
                V.scalar_tensor_tensor(out=wq[:], in0=w_eps, scalar=1.0 / S, in1=w_eps, op0=ALU.mult, op1=ALU.mult,
                                       accum_out=q[:]).then_inc(s["q_ready"], 1)
                V.transpose(wT[:], dw[p][:, t, 0:S]).then_inc(s["wT_ready"], 1)

            link(V.tensor_scalar(vec[:, vcol["conv_w1"], :], vec[:, vcol["conv_w1"], :], 1.0, None, ALU.add))
            assert done[0] == SETUP_VEC
            link(V.tensor_scalar(As[:].rearrange("p a b -> p (a b)"), small[:, 0:2 * S], sm("dt"), None, ALU.mult))
            link(V.tensor_reduce(absrow[:, 0:1], As[:, 0, :], AX_X, ALU.add, apply_absolute_value=True))
            dve.wait_ge(s["pe_setup"], 1)
            link(V.tensor_reduce(absrow[0:1, 1:2], scanP[0:1, 0:S], AX_X, ALU.max))
            dve.wait_ge(s["pe_setup"], 2)
            link(V.tensor_copy(absrow[:, 2:3], scanP[0:S, 0:1]))
            link(V.tensor_scalar(mask[:], sm("pow"), absrow[:, 2:3], None, ALU.is_lt))
            link(V.tensor_scalar(pick[:], mask[:], -1.0, 1.0, ALU.mult, ALU.add))
            link(V.tensor_tensor(pick[:], pick[:], sm("inv"), ALU.add))
            link(V.tensor_reduce(absrow[:, 3:4], pick[:], AX_X, ALU.min))
            link(V.tensor_scalar(absrow[:, 4:5], absrow[:, 3:4], 1.0, None, ALU.min))
            link(V.tensor_scalar(As[:].rearrange("p a b -> p (a b)"), As[:].rearrange("p a b -> p (a b)"),
                                 absrow[:, 4:5], None, ALU.mult))
            link(V.tensor_copy(XX[:, 0, :], ident[0:S, 0:S]))
            assert done[0] == SETUP_SERIES
            for n in range(TERMS, 0, -1):
                dve.wait_ge(s["pe_setup"], 3 + TERMS - n)
                link(V.scalar_tensor_tensor(out=XX[:, 0, :], in0=scanP[0:S, 0:S], scalar=1.0 / n,
                                            in1=ident[0:S, 0:S], op0=ALU.mult, op1=ALU.add))
                for first, stage, src in ((2, 0, xc), (7, 1, xa)):
                    piece = TERMS - n - first
                    if piece == 0:
                        dve.wait_ge(*((s["xa_in"], 16 * NJ) if stage else (s["halo_in"], 16 * B)))
                    if piece in range(NJ):
                        V.bn_stats(stats[:, piece, :], src[:, piece, :]).then_inc(s["stats_done"], 1)
                    if piece == NJ and stage == 0:
                        aggregate(0)
            dve.wait_ge(s["pe_setup"], 3 + TERMS)
            link(V.tensor_copy(XX[:, 1, :], scanP[0:S, 0:S]))
            for n in range(SQUARINGS):
                dve.wait_ge(s["pe_setup"], 4 + TERMS + n)
                link(V.copy_predicated(XX[:].rearrange("p a b -> p (a b)"),
                                       mask[:, n:n + 1].bitcast(I32).to_broadcast([S, 2 * S]),
                                       scanP[0:S, 0:2 * S]))
                if n == 0:
                    aggregate(1)
                if n < 3:
                    if n == 0:
                        dve.wait_ge(s["bt_in"], 16)
                        ins = V.tensor_reduce(btmp[:], BT[:], AX_X, ALU.add)
                    else:
                        dve.wait_ge(s["bt_steps"], n)
                        if n == 1:
                            ins = V.tensor_scalar(btmp[:], btmp[:], -1.0 / S, None, ALU.mult)
                        else:
                            ins = V.tensor_tensor(BT[:], BT[:], btmp[:].unsqueeze(2).to_broadcast([P, KH, S]),
                                                  ALU.add)
                    ins.then_inc(s["bt_steps"], 1)
                if n in DVE_WPRIME:
                    k = DVE_WPRIME.index(n)
                    dve.wait_ge(s["wprime_mm"], k + 1)
                    V.tensor_tensor(WT[:, k, :], WT[:, k, :], wbank[k][:], ALU.add).then_inc(s["wprime_done"], 1)
                if n == DVE_EDGES:
                    dve.wait_ge(s["y_done"], KH)
                    for k in range(KH):
                        V.memset(halo[:, k, :, 0], 0.0)
                        ins = V.memset(halo[:, k, :, 2 * NC + 1], 0.0)
                    ins.then_inc(s["halo_zeroed"], 1)
                if n in DVE_CONV:
                    left_tap(0, DVE_CONV.index(n))
                    right_tap(0, DVE_CONV.index(n), 0)
                if n in DVE_STATS2:
                    bn_stats(2, DVE_STATS2.index(n))
                if n == SQUARINGS - 1:
                    aggregate(2)
                if n in DVE_XG0:
                    gated_x(0, DVE_XG0.index(n), 0)
            link(V.tensor_reduce(absrow[:, 5:6], XX[:, 0, :], AX_X, ALU.add))
            link(V.tensor_scalar(absrow[:, 6:7], absrow[:, 5:6], -1.0 / S, None, ALU.mult))
            link(V.tensor_scalar(AC[:], XX[:, 0, :], absrow[:, 6:7], None, ALU.add))
            link(V.tensor_scalar(M[:], AC[:], sm("st_g"), None, ALU.mult))
            link(V.tensor_scalar(st_b_wide[:], st_b_wide[:], sm("st_b"), None, ALU.mult))
            link(V.tensor_reduce(absrow[0:1, 7:8], Bb[:], AX_X, ALU.add))
            link(V.tensor_scalar(absrow[0:1, 7:8], absrow[0:1, 7:8], -1.0 / S, None, ALU.mult))
            link(V.tensor_scalar(Bb[:], Bb[:], absrow[0:1, 7:8], None, ALU.add))
            assert done[0] == SETUP_M

            for m in range(len(DVE_XG0), KH):
                gated_x(0, m, 0)
            dve.wait_ge(s["pe_setup"], SQ_END + 1)
            link(V.tensor_copy(dbias[:], scanP[0:S, 0:1]))

            def iteration(i, p, parts):
                A, F, C = ("A" in parts), ("F" in parts), ("C" in parts)
                gate_at = V_G if A else V_G_LAST
                for t in range(CT):
                    if F:
                        step(i, p, t)
                    if "S" in parts:
                        if t in V_STATS:
                            bn_stats(i + 3, V_STATS.index(t))
                        if t == V_AGGR:
                            aggregate(i + 3)
                    if A:
                        if t in V_CONV:
                            k, second = divmod(V_CONV.index(t), 2)
                            if second:
                                right_tap(i + 1, k, 1 - p)
                            else:
                                left_tap(i + 1, k)
                        if t in V_XG:
                            gated_x(i + 1, V_XG.index(t), 1 - p)
                    if F:
                        if t in V_SILU:
                            silu(i, V_SILU.index(t), p)
                        if t in gate_at:
                            whole_gate(i, gate_at.index(t), p)
                    if C:
                        if t == V_YS:
                            state_times_c(i - 1, 1 - p)
                        if t in V_SG:
                            gated_ssm(i - 1, V_SG.index(t), 1 - p)
                        if t in V_ADD:
                            add_x(i - 1, V_ADD.index(t))

            iteration(0, 0, "ASF")
            iteration(1, 1, "ASFC")
            with dve.Fori(1, NC // 2 - 1) as pair:
                i = dve.snap(2 * pair)
                iteration(i, 0, "ASFC")
                iteration(i + 1, 1, "ASFC")
            iteration(NC - 2, 0, "AFC")
            iteration(NC - 1, 1, "FC")
            iteration(NC, 0, "C")

        @block.tensor
        def _(pe):
            mm = nc.tensor.matmul
            tp = nc.tensor.transpose

            def fill_z(c, k, i, middle):
                wait_for(pe, "z_done", NJ, c + 1, NJ)
                wait_bank(pe, T_USERS, "z", k, i, middle)
                for j in range(NJ):
                    ins = tp(tbank["z", k][:, P * j:P * j + P], z[:, j, P * k:P * k + P], ident[:])
                ins.then_inc(s["zfill"], 1)

            def fill_x(c, k, i, middle):
                wait_for(pe, "xn_done", NJ, c, NJ)
                wait_bank(pe, T_USERS, "x", k, i, middle)
                for j in range(NJ):
                    ins = tp(tbank["x", k][:, P * j:P * j + P], z[:, j, P * k:P * k + P], ident[:])
                ins.then_inc(s["xfill"], 1)

            def fill_w(c, j, i, middle):
                if j == 0:
                    wait_for(pe, "wr_done", NJ, c, NJ)
                    wait_bank(pe, T_USERS, "wr", 0, i, middle)
                    hold(pe)
                ins = tp(tbank["wr", 0][0:S, P * j:P * j + P], wr[:, j, :], ident[:])
                if j == NJ - 1:
                    ins.then_inc(s["wrfill"], 1)

            def fill_o(c, j, m, i, middle):
                if m == 0:
                    wait_for(pe, "sg_done", KH, c, KH)
                    wait_bank(pe, T_USERS, "o", j, i, middle)
                ins = tp(tbank["o", j][:, P * m:P * m + P], sgT[:, m, P * j:P * j + P], ident[:])
                if m == KH - 1:
                    ins.then_inc(s["ofill"], 1)

            def fill_d(c, j, i, middle):
                if j == 0:
                    wait_for(pe, "dT_done", 1, c, 1)
                    wait_bank(pe, T_USERS, "d", 0, i, middle)
                    hold(pe)
                ins = tp(tbank["d", 0][:, S * j:S * j + S], dT[:, P * j:P * j + P], ident[0:S, 0:S])
                if j == NJ - 1:
                    ins.then_inc(s["dfill"], 1)

            def ffn(c, m, k, i, middle):
                if k == 0:
                    wait_for(pe, "xnT_done", KH, c, KH)
                    wait_bank(pe, M_USERS, "ffn", m, i, middle)
                ins = mm(mbank["ffn", m][:], WT[:, k, P * m:P * m + P], xnT[:, k, :],
                         start=(k == 0), stop=(k == KH - 1))
                if k == KH - 1:
                    ins.then_inc(s["ffn_mm"], 1)

            def gate(c, m, k, p, i, middle):
                if k == 0:
                    wait_bank(pe, M_USERS, "gate", m, i, middle)
                ins = mm(mbank["gate", m][:], gateT[:, k, P * m:P * m + P], xnorm[p][:, k, :],
                         start=(k == 0), stop=(k == KH - 1))
                if k == KH - 1:
                    ins.then_inc(s["gate_mm"], 1)

            def in_gate(c, m, k, p, i, middle):
                if k == 0:
                    wait_for(pe, "xnorm_done", KH, c, KH)
                    wait_bank(pe, M_USERS, "ig", m, i, middle)
                ins = mm(mbank["ig", m][:], gateT[:, k, H + P * m:H + P * m + P], xnorm[p][:, k, :],
                         start=(k == 0), stop=(k == KH - 1))
                if k == KH - 1:
                    ins.then_inc(s["ig_mm"], 1)

            def b_proj(c, k, i, middle):
                if k == 0:
                    wait_bank(pe, M_USERS, "b", 0, i, middle)
                wait_for(pe, "xg_done", KH, c, k + 1)
                ins = mm(mbank["b", 0][0:S, :], BT[:, k, :], xg[:, k, :], start=(k == 0), stop=(k == KH - 1))
                if k == KH - 1:
                    ins.then_inc(s["b_mm"], 1)

            def c_proj(c, k, p, i, middle):
                if k == 0:
                    wait_bank(pe, M_USERS, "c", 0, i, middle)
                ins = mm(mbank["c", 0][0:S, :], CwT[:, k, :], xnorm[p][:, k, :],
                         start=(k == 0), stop=(k == KH - 1))
                if k == KH - 1:
                    ins.then_inc(s["c_mm"], 1)

            def ssm(c, m, i, middle):
                if m == 0:
                    wait_for(pe, "ys_done", 1, c, 1)
                wait_bank(pe, M_USERS, "ssm", m, i, middle)
                mm(mbank["ssm", m][:], DT[:, P * m:P * m + P], ys[:],
                   start=True, stop=True).then_inc(s["ssm_mm"], 1)

            def step(i, t):
                wait_for(pe, "wT_ready", CT, i, t + 1)
                hold(pe)
                mm(scanP[0:B, 0:S], wT[:, 0:B], M2[:, 0, :], start=True, stop=False)
                mm(scanP[0:B, 0:S], wT[:, 32:32 + B], M2[:, 1, :], start=False, stop=True
                   ).then_inc(s["p_ready"], 1)

            pe.wait_ge(s["consts"], 16 * 4)
            pe.wait_ge(s["dve_setup"], SETUP_VEC + 2)
            tp(scanP[0:1, 0:S], absrow[:, 0:1], ident[0:S, 0:S]).then_inc(s["pe_setup"], 1)
            pe.wait_ge(s["dve_setup"], SETUP_VEC + 3)
            mm(scanP[0:S, 0:1], ones[0:1, 0:S], absrow[0:1, 1:2], start=True, stop=True
               ).then_inc(s["pe_setup"], 1)
            for n in range(TERMS):
                pe.wait_ge(s["dve_setup"], SETUP_SERIES + n)
                mm(scanP[0:S, 0:S], As[:, 1, :], XX[:, 0, :], start=True, stop=True
                   ).then_inc(s["pe_setup"], 1)
            pe.wait_ge(s["dve_setup"], SETUP_SERIES + TERMS)
            tp(scanP[0:S, 0:S], XX[:, 0, :], ident[0:S, 0:S]).then_inc(s["pe_setup"], 1)
            for n in range(SQUARINGS):
                pe.wait_ge(s["dve_setup"], SETUP_SERIES + TERMS + 1 + n)
                mm(scanP[0:S, 0:S], XX[:, 1, :], XX[:, 0, :], start=True, stop=True)
                mm(scanP[0:S, S:2 * S], XX[:, 0, :], XX[:, 1, :], start=True, stop=True
                   ).then_inc(s["pe_setup"], 1)
                for k in range(KH):
                    if PE_HALO[k] == n:
                        fill_z(-1, k, -2, False)
                    if PE_Z0[k] == n:
                        fill_z(0, k, -1, False)
                if n in PE_WPRIME:
                    k = PE_WPRIME.index(n)
                    pe.wait_ge(s["weights_in"], 16 * 3)
                    if k >= 2:
                        pe.wait_ge(s["wprime_done"], k - 1)
                    mm(wbank[k][:], VT[:, P * k:P * k + P], CrT[:], start=True, stop=True
                       ).then_inc(s["wprime_mm"], 1)
                if n == PE_IG0[0]:
                    pe.wait_ge(s["gate_in"], 16 * 3)
                for piece, at in enumerate(PE_IG0):
                    if at == n:
                        in_gate(0, *divmod(piece, KH), 0, -1, False)
                for k in range(KH):
                    if PE_X0[k] == n:
                        fill_x(0, k, -1, False)
            for piece in range(len(PE_IG0), KH * KH):
                in_gate(0, *divmod(piece, KH), 0, -1, False)
            pe.wait_ge(s["bt_steps"], 3)
            for k in range(KH - 1):
                b_proj(0, k, -1, False)
            pe.wait_ge(s["dve_setup"], SETUP_M)
            mm(scanP[0:S, 0:1], AC[:], sm("st_b"), start=True, stop=False)
            mm(scanP[0:S, 0:1], Bb[:], ones[0:1, 0:1], start=False, stop=True).then_inc(s["pe_setup"], 1)
            b_proj(0, KH - 1, -1, False)
            pe.wait_ge(s["dve_setup"], SETUP_M + 1)
            mm(scanP[0:B, 0:S], st_b_wide[:, 0:B], AC[:], start=True, stop=True).then_inc(s["p_ready"], 1)
            for j in range(NJ):
                fill_d(0, j, -1, False)
            for k in range(KH):
                c_proj(0, k, 0, -1, False)
            pe.wait_ge(s["wprime_done"], KH)
            pe.wait_ge(s["m2_in"], 32)

            def iteration(i, p, parts, middle):
                A, F, C = ("A" in parts), ("F" in parts), ("C" in parts)
                gate_at = PE_GATE if A else PE_GATE_LAST
                in_gate_at = PE_IG if C else PE_IG_FIRST
                for t in range(CT):
                    if F:
                        step(i, t)
                        if t in PE_FFN:
                            ffn(i, *divmod(PE_FFN.index(t), KH), i, middle)
                    if C:
                        if t in PE_W:
                            fill_w(i - 1, PE_W.index(t), i, middle)
                        if t in PE_SSM:
                            ssm(i - 1, PE_SSM.index(t), i, middle)
                    if A:
                        for k in range(KH):
                            if PE_Z[k] == t:
                                fill_z(i + 1, k, i, middle)
                            if PE_X[k] == t:
                                fill_x(i + 1, k, i, middle)
                    if F and t in gate_at:
                        m, k = divmod(gate_at.index(t), KH)
                        gate(i, m, k, p, i, middle)
                    if C and t in PE_O:
                        fill_o(i - 1, *divmod(PE_O.index(t), KH), i, middle)
                    if A:
                        if t in in_gate_at:
                            in_gate(i + 1, *divmod(in_gate_at.index(t), KH), 1 - p, i, middle)
                        if t in PE_B:
                            b_proj(i + 1, PE_B.index(t), i, middle)
                        if t in PE_D:
                            fill_d(i + 1, PE_D.index(t), i, middle)
                        if t in PE_C:
                            c_proj(i + 1, PE_C.index(t), 1 - p, i, middle)

            iteration(0, 0, "ASF", False)
            iteration(1, 1, "ASFC", False)
            with pe.Fori(1, NC // 2 - 1) as pair:
                i = pe.snap(2 * pair)
                iteration(i, 0, "ASFC", True)
                iteration(i + 1, 1, "ASFC", True)
            iteration(NC - 2, 0, "AFC", False)
            iteration(NC - 1, 1, "FC", False)
            iteration(NC, 0, "C", False)


LN_OPS = 12
SETUP_VEC = 1
SETUP_SERIES = SETUP_VEC + 11
SETUP_M = SETUP_SERIES + TERMS + 1 + SQUARINGS + 8
SQ_END = 3 + TERMS + SQUARINGS


def kernel(**inputs):
    import concourse.bacc as _bacc
    from concourse.bass_utils import run_bass_kernel_spmd as _run

    a = {k: np.asarray(v) for k, v in inputs.items()}
    at = {k[len("L0_attn_"):]: v for k, v in a.items() if k.startswith("L0_attn_")}
    blocks = lambda v: v.reshape(KH, P).T
    conv = at["conv_w"].reshape(H, 3)
    parts = {"ln_g": at["ln_in_g"], "ln_b": at["ln_in_b"], "conv_w0": conv[:, 0], "conv_w1": conv[:, 1],
             "conv_w2": conv[:, 2], "conv_b": at["conv_b"], "gate_b": at["gate_b"][:H],
             "in_gate_b": at["gate_b"][H:], "ffn_b": a["L0_ffn_b"], "D_b": at["D_b"]}
    vec = np.stack([blocks(parts[n]) for n in VEC], axis=1)
    powers = np.float32(2.0) ** np.arange(SQUARINGS, dtype=np.float32)
    halves = np.float32(0.5) ** np.arange(1, SQUARINGS + 1, dtype=np.float32)
    small = np.concatenate([
        at["A"], at["A"].T, at["ln_st_g"][:, None], at["ln_st_b"][:, None], at["C_b"][:, None],
        np.broadcast_to(at["dt_A"].reshape(1, 1), (S, 1)),
        np.broadcast_to(powers, (S, SQUARINGS)), np.broadcast_to(halves, (S, SQUARINGS))], axis=1)
    arrays = {
        "x": at["x"], "ident": np.eye(P, dtype=np.float32), "gateT": at["gate_w"].T, "WT": a["L0_ffn_W"].T,
        "VT": a["L0_ffn_V_r"].T, "CrT": a["L0_ffn_C"].T, "BT": at["B_w"].T, "CwT": at["C_w"].T,
        "DT": at["D_w"].T, "vec": vec, "small": small, "Bb": at["B_b"].reshape(1, S),
    }
    nc = _bacc.Bacc("TRN2", target_bir_lowering=False, num_devices=1)
    held, args = {}, []
    for name, v in arrays.items():
        v = np.ascontiguousarray(v)
        held[f"in_{name}"] = v
        args.append(nc.dram_tensor(f"in_{name}", v.shape, mybir.dt.from_np(v.dtype), kind="ExternalInput").ap())
    out = nc.dram_tensor("out_0", (B, T, H), F32, kind="ExternalOutput").ap()
    build(nc, *args, out)
    r = _run(nc, [held], core_ids=[0])
    return r.results[0]["out_0"]
```
